# Optimizing a Trainium2 kernel written in Bass

```python
import numpy as np
import jax
import jax.numpy as jnp

def _softmax(x, axis=-1):
    return jax.nn.softmax(x, axis=axis)

def _gelu(x):
    return jax.nn.gelu(x, approximate=True)

def _silu(x):
    return jax.nn.silu(x)

def _sigmoid(x):
    return jax.nn.sigmoid(x)

def _layernorm(x, axis=-1, eps=1e-05):
    m = jnp.mean(x, axis=axis, keepdims=True)
    v = jnp.var(x, axis=axis, keepdims=True)
    return (x - m) / jnp.sqrt(v + eps)

def _scatter_add(tgt, idx, src, axis=0):
    return tgt.at[idx].add(src)

def _segment_sum(src, seg, n):
    return jax.ops.segment_sum(src, seg, n)
kernel_name = 'mk_adj_ffn_d1_adj_r2_437445'

def setup_inputs(seed: int=0):
    np.random.seed(seed)
    _w = jnp.asarray

    def _rec_inputs():
        import jax
        import jax.numpy as jnp
        _gk = jax.random.key(seed)
        x = -0.0002928 + 1 * jax.random.normal(jax.random.fold_in(_gk, 1), (2048, 512), jnp.float32)
        _a = jax.random.bernoulli(jax.random.fold_in(_gk, 2), 0.0078125, (2048, 2048))
        _af = _a.astype(jnp.float32)
        adj = _af
        return (x, adj)
    x, adj = _rec_inputs()

    def _L0_gnn_setup():
        import jax, jax.numpy as jnp
        import numpy as np
        N = 2048
        D_IN = 512
        H = 16
        DH = D_IN // H
        ALPHA = 0.2
        MASK_VAL = -65500.0
        key = jax.random.key(seed)
        ks = jax.random.split(key, 7)
        x = jax.random.normal(ks[0], (N, D_IN), dtype=jnp.float32)
        adj = jax.random.randint(ks[1], (N, N), 0, 2).astype(jnp.float32)
        s = 1.0 / np.sqrt(D_IN)
        W_seq = jax.random.normal(ks[2], (D_IN, D_IN), dtype=jnp.float32) * s
        a1 = jax.random.normal(ks[3], (DH,), dtype=jnp.float32) / np.sqrt(DH)
        a2 = jax.random.normal(ks[4], (DH,), dtype=jnp.float32) / np.sqrt(DH)
        W_out = jax.random.normal(ks[5], (D_IN, D_IN), dtype=jnp.float32) * s
        b_out = jax.random.normal(ks[6], (D_IN,), dtype=jnp.float32) * 0.01
        return {'x': x, 'adj': adj, 'W_seq': W_seq, 'a1': a1, 'a2': a2, 'W_out': W_out, 'b_out': b_out}
    _L0_gnn_all = _L0_gnn_setup()
    _L0_gnn_in = {k: v for k, v in _L0_gnn_all.items() if k in ('W_seq', 'a1', 'a2', 'W_out', 'b_out')}
    del _L0_gnn_all

    def _L0_ffn_setup():
        import jax, jax.numpy as jnp
        import numpy as np
        DIM = 512
        LATENT = 256
        INTER = 256
        SHARED = 2048
        E = 8
        TOPK = 2
        NGROUP = 2
        TOPKG = 1
        NORM_TOPK = True
        SCALE = 1.0
        B, S = (2, 512)

        def relu2(x):
            r = jnp.maximum(x, 0.0)
            return r * r
        key = jax.random.key(seed)
        ks = jax.random.split(key, 8)

        def w(k, shape, std=0.02):
            return jax.random.normal(k, shape, dtype=jnp.float32) * std
        return {'x': jax.random.normal(ks[0], (B, S, DIM), dtype=jnp.float32), 'gate': w(ks[1], (E, DIM)), 'corr_bias': jnp.zeros((E,), jnp.float32), 'w1': w(ks[2], (E, INTER, LATENT)), 'w2': w(ks[3], (E, LATENT, INTER)), 'fc1_w': w(ks[4], (LATENT, DIM)), 'fc2_w': w(ks[5], (DIM, LATENT)), 'up_w': w(ks[6], (SHARED, DIM)), 'down_w': w(ks[7], (DIM, SHARED))}
    _L0_ffn_all = _L0_ffn_setup()
    _L0_ffn_in = {k: v for k, v in _L0_ffn_all.items() if k in ('gate', 'corr_bias', 'w1', 'w2', 'fc1_w', 'fc2_w', 'up_w', 'down_w')}
    del _L0_ffn_all
    return {'x': x, 'adj': adj, 'L0_gnn_W_seq': _L0_gnn_in['W_seq'], 'L0_gnn_a1': _L0_gnn_in['a1'], 'L0_gnn_a2': _L0_gnn_in['a2'], 'L0_gnn_W_out': _L0_gnn_in['W_out'], 'L0_gnn_b_out': _L0_gnn_in['b_out'], 'L0_ffn_gate': _L0_ffn_in['gate'], 'L0_ffn_corr_bias': _L0_ffn_in['corr_bias'], 'L0_ffn_w1': _L0_ffn_in['w1'], 'L0_ffn_w2': _L0_ffn_in['w2'], 'L0_ffn_fc1_w': _L0_ffn_in['fc1_w'], 'L0_ffn_fc2_w': _L0_ffn_in['fc2_w'], 'L0_ffn_up_w': _L0_ffn_in['up_w'], 'L0_ffn_down_w': _L0_ffn_in['down_w']}

def reference(x, adj, L0_gnn_W_seq, L0_gnn_a1, L0_gnn_a2, L0_gnn_W_out, L0_gnn_b_out, L0_ffn_gate, L0_ffn_corr_bias, L0_ffn_w1, L0_ffn_w2, L0_ffn_fc1_w, L0_ffn_fc2_w, L0_ffn_up_w, L0_ffn_down_w):
    import jax
    import jax.numpy as jnp

    def _L0_gnn_ref(x, adj, W_seq, a1, a2, W_out, b_out):
        import jax, jax.numpy as jnp
        import numpy as np
        N = 2048
        D_IN = 512
        H = 16
        DH = D_IN // H
        ALPHA = 0.2
        MASK_VAL = -65500.0
        seq = (x @ W_seq).reshape(N, H, DH)
        score1 = jnp.einsum('nhd,d->hn', seq, a1)
        score2 = jnp.einsum('nhd,d->hn', seq, a2)
        scores = score1[:, :, None] + score2[:, None, :]
        scores = jax.nn.leaky_relu(scores, negative_slope=ALPHA)
        scores = scores + (1.0 - adj)[None, :, :] * MASK_VAL
        attn = jax.nn.softmax(scores, axis=-1)
        hidden = jnp.einsum('hij,jhd->ihd', attn, seq).reshape(N, D_IN)
        hidden = hidden @ W_out + b_out
        return jax.nn.elu(hidden)

    def _L0_ffn_ref(x, gate, corr_bias, w1, w2, fc1_w, fc2_w, up_w, down_w):
        import jax, jax.numpy as jnp
        import numpy as np
        DIM = 512
        LATENT = 256
        INTER = 256
        SHARED = 2048
        E = 8
        TOPK = 2
        NGROUP = 2
        TOPKG = 1
        NORM_TOPK = True
        SCALE = 1.0
        B, S = (2, 512)

        def relu2(x):
            r = jnp.maximum(x, 0.0)
            return r * r
        Bv, Sv, D = x.shape
        xf = x.reshape(-1, D)
        N = xf.shape[0]
        scores = jax.nn.sigmoid(xf.astype(jnp.float32) @ gate.T)
        sfc = scores + corr_bias
        gs = E // NGROUP
        if NGROUP > 1:
            group_scores = jax.lax.top_k(sfc.reshape(N, NGROUP, gs), 2)[0].sum(-1)
            gidx = jax.lax.top_k(group_scores, TOPKG)[1]
            gmask = jnp.zeros((N, NGROUP), sfc.dtype).at[jnp.arange(N)[:, None], gidx].set(1.0)
            smask = jnp.repeat(gmask, gs, axis=1)
            sfc = jnp.where(smask > 0, sfc, 0.0)
        sel = jax.lax.top_k(sfc, TOPK)[1]
        top_scores = jnp.take_along_axis(scores, sel, axis=1)
        if NORM_TOPK:
            top_scores = top_scores / (top_scores.sum(-1, keepdims=True) + 1e-20)
        flat = sel.reshape(-1)
        perm = jnp.argsort(flat, stable=True)
        sorted_eid = flat[perm]
        scores_sorted = top_scores.reshape(-1)[perm]
        tok = perm // TOPK
        lat = xf @ fc1_w.T
        xs = lat[tok]
        out = jnp.zeros_like(xs)
        for e in range(E):
            he = relu2(xs @ w1[e].T) @ w2[e].T
            out = jnp.where((sorted_eid == e)[:, None], he, out)
        out = out * scores_sorted[:, None]
        comb = jnp.zeros((N, LATENT), out.dtype).at[tok].add(out)
        routed = comb @ fc2_w.T * SCALE
        shared = relu2(xf @ up_w.T) @ down_w.T
        return (routed + shared).reshape(Bv, Sv, D)
    x = x + _L0_gnn_ref(_layernorm(x, axis=-1), adj, L0_gnn_W_seq, L0_gnn_a1, L0_gnn_a2, L0_gnn_W_out, L0_gnn_b_out)
    x = x + _L0_ffn_ref(_layernorm(x, axis=-1)[None], L0_ffn_gate, L0_ffn_corr_bias, L0_ffn_w1, L0_ffn_w2, L0_ffn_fc1_w, L0_ffn_fc2_w, L0_ffn_up_w, L0_ffn_down_w)[0]
    return x

_drawn_inputs = setup_inputs


def setup_inputs(seed=0):
    import zlib

    import numpy as np

    out = dict(_drawn_inputs(seed))
    spreads = {'L0_ffn_corr_bias': (0.0, 0.8)}
    factors = {'L0_gnn_b_out': 6.335,
     'L0_ffn_gate': 8.0,
     'L0_ffn_w1': 8.0,
     'L0_ffn_w2': 8.0,
     'L0_ffn_fc1_w': 8.0,
     'L0_ffn_fc2_w': 8.0,
     'L0_ffn_up_w': 8.0,
     'L0_ffn_down_w': 8.0}
    for name, (base, spread) in spreads.items():
        noise = np.random.default_rng([zlib.crc32(name.encode()), seed]).standard_normal(out[name].shape)
        drawn = base * np.exp(spread * noise) if base else spread * noise
        out[name] = jnp.asarray(drawn.astype(out[name].dtype))
    for name, factor in factors.items():
        out[name] = (out[name] * factor).astype(out[name].dtype)
    return out
```

```python
from contextlib import ExitStack

import concourse.bass as bass
from concourse import mybir

f32 = mybir.dt.float32
f16 = mybir.dt.float16
f8 = mybir.dt.float8e4
u8 = mybir.dt.uint8
u32 = mybir.dt.uint32
ALU = mybir.AluOpType
ACT = mybir.ActivationFunctionType
AX = mybir.AxisListType

P = 128
N = 2048
D = 512
H = 16
DH = D // H
T = N // P
KD = D // P
W1 = DH + 1
WD = 2 * W1
WV = 2 * WD
IC = 1024
IT = IC // P
NIC = N // IC
UNITS = H * NIC
DVE_J = 6
E, LAT, INTER, SH = 8, 256, 256, 2048
TC = 512
NC_ = N // TC
TT = TC // P
KL, KI, FS = LAT // P, INTER // P, SH // P
EPS = 1e-5
ALPHA = 0.2
STEEP = 2.0 ** 60
ONE8, NEG8 = 56, 184
VTOP = 2.0 ** 14


def build(nc, x, adjT, w_seq, a1, a2, w_out, b_out, gateT, corr, w1T, w2T, fc1T, fc2T, upT, downT,
          ident_in, lower_in, out):
    s1_dram = nc.dram_tensor("s1_rows", (H, N), f32, kind="Internal").ap()
    w_dram = nc.dram_tensor("expert_weight_rows", (E, N), f32, kind="Internal").ap()
    ctx = ExitStack()
    with ctx:
        def sem(name):
            return ctx.enter_context(nc.semaphore(name))

        arena = ctx.enter_context(nc.sbuf_tensor("arena", [P, 53200], f32))
        bank = [ctx.enter_context(nc.psum_tensor(f"bank{i}", [P, 512], f32)) for i in range(8)]

        def at(off, words, dt=f32):
            v = arena[:, off:off + words]
            return v if dt == f32 else v.bitcast(dt)

        O_ADJ, O_VB, O_M, O_HID, O_VS, O_S1B, O_SUM = 0, 8192, 25088, 33280, 41728, 43840, 45888
        O_SMALL = O_SUM + 4 * IT * WD
        adj8 = at(O_ADJ, 8192, f8).rearrange("p (j i) -> p j i", j=T)
        adjw = at(O_ADJ, 8192, u32).rearrange("p (j i) -> p j i", j=T)
        vb = at(O_VB, 16896, f16).rearrange("p (h j c) -> p h j c", h=H, j=T)
        x_sb = at(O_VB, 8192).rearrange("p (t d) -> p t d", t=T)
        xnT = at(O_VB + 8192, 8192).rearrange("p (k n) -> p k n", k=KD)
        m8 = at(O_M, 8192, f8).rearrange("p (b j i) -> p b j i", b=NIC, j=T)
        mu8 = at(O_M, 8192, u8).rearrange("p (b j i) -> p b j i", b=NIC, j=T)
        mw = at(O_M, 8192, u32).rearrange("p (b j i) -> p b j i", b=NIC, j=T)
        adj_in = at(O_M, 8192).rearrange("p (b i) -> p b i", b=4)
        hid = at(O_HID, T * H * W1).rearrange("p (t h c) -> p t h c", t=T, h=H)
        v_sb = at(O_HID, T * D).rearrange("p (t d) -> p t d", t=T)
        wa_tmp = at(O_HID, KD * D).rearrange("p (a c) -> p a c", c=DH)
        vs = at(O_VS, 2112, f16).rearrange("p (b j c) -> p b j c", b=2, j=T)
        vtmp = at(O_VS, 2112).rearrange("p (b j c) -> p b j c", b=2, j=T)
        s1b = at(O_S1B, 2048).rearrange("p (b i) -> p b i", b=NIC)
        wseq_sb = at(O_S1B, 2048).rearrange("p (k n) -> p k n", k=KD)
        sums = at(O_SUM, 2 * IT * WD).rearrange("p (b t c) -> p b t c", b=2, t=IT)
        scaled = at(O_SUM + 2 * IT * WD, 2 * IT * WD).rearrange("p (b t c) -> p b t c", b=2, t=IT)
        s1T = at(O_SUM, N)[0:H, :]
        top = [O_SMALL]

        def small(words, dt=f32):
            top[0] += words
            assert top[0] <= 53200
            return at(top[0] - words, words, dt)

        ident = small(P)
        ones16 = small(P // 2, f16)
        flag8 = small(N // 4, u8)
        flagw = flag8.bitcast(u32)
        s_nat = small(T * 2 * H).rearrange("p (t s) -> p t s", t=T)
        bval = small(T * H).rearrange("p (t h) -> p t h", t=T)
        nval = small(T * H).rearrange("p (t h) -> p t h", t=T)
        zval = small(T * H).rearrange("p (t h) -> p t h", t=T)
        zneg = small(T * H).rearrange("p (t h) -> p t h", t=T)
        neg_s2 = small(H * T).rearrange("p (h t) -> p h t", h=H)
        step_bias = small(H * T).rearrange("p (h t) -> p h t", h=H)
        bias_now = small(2 * T).rearrange("p (b t) -> p b t", b=2)
        coef = small(H * T * 2).rearrange("p (h t c) -> p h t c", h=H, t=T)
        wa = small(KD * 2 * H).rearrange("p (k s) -> p k s", k=KD)
        a_sb = small(2 * DH).rearrange("p (s d) -> p s d", s=2)
        stat6 = small(4 * 6).rearrange("p (t c) -> p t c", t=4)
        mv = small(T * 2).rearrange("p (t c) -> p t c", t=T)
        std = small(T)
        rstd = small(T)
        vmx = small(T)
        tops = small(H + 1)
        topr = small(H + 1)
        gfac = small(4)

        x_loaded = [sem(f"x_loaded{g}") for g in range(4)]
        adj_loaded = [sem(f"adj_loaded{g}") for g in range(4)]
        consts_loaded, wseq_loaded = sem("consts_loaded"), sem("wseq_loaded")
        dve_step, act_step, pool_step = sem("dve_step"), sem("act_step"), sem("pool_step")
        wa_ready, var_ready, std_ready, xn_ready = sem("wa_ready"), sem("var_ready"), sem("std_ready"), sem("xn_ready")
        xt_in_psum, xt_copied, seq_in_psum, v_copied = sem("xt_in_psum"), sem("xt_copied"), sem("seq_in_psum"), sem("v_copied")
        s_copied, s1t_in_psum, s1t_copied, s1_stored = sem("s_copied"), sem("s1t_in_psum"), sem("s1t_copied"), sem("s1_stored")
        tops_ready, topr_ready, expin_ready, exp_ready = sem("tops_ready"), sem("topr_ready"), sem("expin_ready"), sem("exp_ready")
        ones_ready, bn_ready, dpart_ready, bpart_ready, hi_ready = sem("ones_ready"), sem("bn_ready"), sem("dpart_ready"), sem("bpart_ready"), sem("hi_ready")
        lo_done, adj_cast, deg_in_psum = sem("lo_done"), sem("adj_cast"), sem("deg_in_psum")

        with nc.Block() as block:
            @block.sync
            def _(sp):
                for g in range(4):
                    sp.dma_start(x_sb[:, 4 * g:4 * g + 4, :],
                                 x[512 * g:512 * g + 512, :].rearrange("(t p) d -> p t d", p=P)
                                 ).then_inc(x_loaded[g], 16)
                for n in range(T):
                    if n >= 4:
                        sp.wait_ge(adj_cast, n - 3)
                    sp.dma_start(adj_in[:, n % 4, :], adjT[n * P:(n + 1) * P, :]).then_inc(adj_loaded[n % 4], 16)
                sp.wait_ge(s1t_copied, 4)
                sp.dma_start(s1_dram[:, :], s1T).then_inc(s1_stored, 16)
                sp.wait_ge(s1_stored, 16)

            @block.scalar
            def _(act):
                act.dma_start(wseq_sb, w_seq.rearrange("(k p) n -> p k n", p=P)).then_inc(wseq_loaded, 16)
                act.dma_start(a_sb[:, 0, :], a1[None, :].to_broadcast([P, DH])).then_inc(consts_loaded, 16)
                act.dma_start(a_sb[:, 1, :], a2[None, :].to_broadcast([P, DH])).then_inc(consts_loaded, 16)
                act.dma_start(ident, ident_in[:, :]).then_inc(consts_loaded, 16)

                def copy_v(t):
                    act.wait_ge(seq_in_psum, t + 1)
                    nc.scalar.copy(v_sb[:, t, :], bank[2 + t % 2][:, :]).then_inc(v_copied, 1)

                for g in range(4):
                    act.wait_ge(var_ready, g + 1)
                    nc.scalar.activation(std[:, 4 * g:4 * g + 4], std[:, 4 * g:4 * g + 4], ACT.Sqrt).then_inc(std_ready, 1)
                    for t in range(4 * g, 4 * g + 4):
                        act.wait_ge(xt_in_psum, t + 1)
                        nc.scalar.copy(xnT[:, :, t * P:(t + 1) * P],
                                       bank[t % 2][:, :].rearrange("p (k n) -> p k n", k=KD)).then_inc(xt_copied, 1)
                        if t >= 1:
                            copy_v(t - 1)
                copy_v(T - 1)
                for c in range(4):
                    act.wait_ge(s1t_in_psum, c + 1)
                    nc.scalar.copy(s1T[:, c * 512:(c + 1) * 512], bank[c % 2][0:H, :]).then_inc(s1t_copied, 1)
                act.wait_ge(expin_ready, 1)
                nc.scalar.activation(coef.rearrange("p h t c -> p t h c")[:, :, :, 0], zval, ACT.Exp)
                nc.scalar.activation(coef.rearrange("p h t c -> p t h c")[:, :, :, 1], zneg, ACT.Exp)
                nc.scalar.activation(bval, nval, ACT.Exp).then_inc(act_step, 1)
                act.wait_ge(act_step, 1)
                nc.scalar.activation(nval, nval, ACT.Exp, scale=ALPHA).then_inc(exp_ready, 1)
                for h in range(H):
                    act.wait_ge(bpart_ready, h + 1)
                    act.wait_ge(dpart_ready, h + 1)
                    nc.scalar.copy(vb[:, h, :, 0:WD], vtmp[:, h % 2, :, :]).then_inc(hi_ready, 1)

            @block.gpsimd
            def _(pool):
                nc.gpsimd.memset(ones16, 1.0).then_inc(ones_ready, 1)
                pool.wait_ge(tops_ready, 1)
                nc.gpsimd.partition_all_reduce(topr, tops, P, bass.bass_isa.ReduceOp.max).then_inc(topr_ready, 1)
                pool.wait_ge(bn_ready, 1)
                for h in range(H):
                    if h >= 2:
                        pool.wait_ge(lo_done, h - 1)
                    nc.gpsimd.tensor_tensor(vtmp[:, h % 2, :, W1:W1 + DH], v_sb[:, :, h * DH:(h + 1) * DH],
                                            nval[:, :, h:h + 1].to_broadcast([P, T, DH]), ALU.mult)
                    nc.gpsimd.tensor_copy(vtmp[:, h % 2, :, WD - 1:WD], nval[:, :, h:h + 1]).then_inc(dpart_ready, 1)

            @block.vector
            def _(dve):
                steps = [0]

                def step(ins):
                    steps[0] += 1
                    ins.then_inc(dve_step, 1)
                    dve.wait_ge(dve_step, steps[0])

                dve.wait_ge(wseq_loaded, 16)
                dve.wait_ge(consts_loaded, 48)
                for s in range(2):
                    step(nc.vector.tensor_tensor(wa_tmp, wseq_sb.rearrange("p k (h d) -> p (k h) d", d=DH),
                                                 a_sb[:, s:s + 1, :].to_broadcast([P, KD * H, DH]), ALU.mult))
                    step(nc.vector.reduce_sum(wa[:, :, s * H:(s + 1) * H],
                                              wa_tmp.rearrange("p (k h) d -> p k h d", k=KD), AX.X))
                dve.sem_inc(wa_ready, 1)
                for g in range(4):
                    dve.wait_ge(x_loaded[g], 16)
                    for t in range(4 * g, 4 * g + 4):
                        step(nc.vector.bn_stats(stat6[:, t % 4, :], x_sb[:, t, :]))
                        step(nc.vector.bn_aggr(mv[:, t, :], stat6[:, t % 4, :]))
                    nc.vector.tensor_scalar(std[:, 4 * g:4 * g + 4], mv[:, 4 * g:4 * g + 4, 1], EPS, None,
                                            ALU.add).then_inc(var_ready, 1)
                    dve.wait_ge(std_ready, g + 1)
                    step(nc.vector.reciprocal(rstd[:, 4 * g:4 * g + 4], std[:, 4 * g:4 * g + 4]))
                    for t in range(4 * g, 4 * g + 4):
                        nc.vector.tensor_scalar(x_sb[:, t, :], x_sb[:, t, :], mv[:, t, 0:1], rstd[:, t:t + 1],
                                                ALU.subtract, ALU.mult).then_inc(xn_ready, 1)
                for t in range(T):
                    dve.wait_ge(v_copied, t + 1)
                    last = nc.vector.reduce_max(vmx[:, t:t + 1], v_sb[:, t, :], AX.X, apply_absolute_value=True)
                step(last)
                nc.vector.reduce_max(tops[:, H:H + 1], vmx, AX.X)
                dve.wait_ge(seq_in_psum, T)
                nc.vector.tensor_copy(s_nat, bank[4][:, :].rearrange("p (t s) -> p t s", t=T)).then_inc(s_copied, 1)
                dve.wait_ge(s_copied, 1)
                nc.vector.reduce_max(tops[:, 0:H], s_nat[:, :, H:].rearrange("p t h -> p h t"), AX.X).then_inc(tops_ready, 1)
                nc.vector.tensor_scalar(neg_s2, s_nat[:, :, H:].rearrange("p t h -> p h t"), -1.0, None, ALU.mult)
                nc.vector.tensor_scalar(step_bias, s_nat[:, :, H:].rearrange("p t h -> p h t"), STEEP, None, ALU.mult)
                dve.wait_ge(topr_ready, 1)
                topb = topr[:, None, 0:H].to_broadcast([P, T, H])
                step(nc.vector.tensor_tensor(zval, s_nat[:, :, 0:H], topb, ALU.add))
                step(nc.vector.tensor_scalar(zneg, zval, -(1 - ALPHA), 0.0, ALU.mult, ALU.min))
                step(nc.vector.tensor_scalar(zval, zval, 1 - ALPHA, 0.0, ALU.mult, ALU.min))
                nc.vector.tensor_tensor(nval, s_nat[:, :, H:], topb, ALU.subtract).then_inc(expin_ready, 1)
                step(nc.vector.tensor_scalar(gfac[:, 0:1], topr[:, H:H + 1], 1.0, None, ALU.max))
                step(nc.vector.reciprocal(gfac[:, 1:2], gfac[:, 0:1]))
                step(nc.vector.tensor_scalar(gfac[:, 2:3], gfac[:, 1:2], VTOP, None, ALU.mult))
                step(nc.vector.tensor_scalar(gfac[:, 3:4], gfac[:, 1:2], -VTOP, None, ALU.mult))
                dve.wait_ge(exp_ready, 1)
                step(nc.vector.tensor_scalar(bval, bval, gfac[:, 2:3], None, ALU.mult))
                nc.vector.tensor_scalar(nval, nval, gfac[:, 3:4], None, ALU.mult).then_inc(bn_ready, 1)

                def branch_b(h):
                    if h >= 2:
                        dve.wait_ge(hi_ready, h - 1)
                        dve.wait_ge(lo_done, h - 1)
                    nc.vector.tensor_tensor(vtmp[:, h % 2, :, 0:DH], v_sb[:, :, h * DH:(h + 1) * DH],
                                            bval[:, :, h:h + 1].to_broadcast([P, T, DH]), ALU.mult)
                    nc.vector.tensor_copy(vtmp[:, h % 2, :, DH:W1], bval[:, :, h:h + 1]).then_inc(bpart_ready, 1)

                branch_b(0)
                for h in range(H):
                    if h + 1 < H:
                        branch_b(h + 1)
                    dve.wait_ge(adj_loaded[h % 4], 16 * (h // 4 + 1))
                    nc.vector.tensor_scalar(adj8[:, h, :], adj_in[:, h % 4, :], -1.0, None, ALU.mult,
                                            saturate=False).then_inc(adj_cast, 1)
                    dve.wait_ge(hi_ready, h + 1)
                    nc.vector.tensor_tensor(vb[:, h, :, WD:], vtmp[:, h % 2, :, :], vb[:, h, :, 0:WD],
                                            ALU.subtract).then_inc(lo_done, 1)
                for c in range(4):
                    dve.wait_ge(deg_in_psum, c + 1)
                    last = nc.vector.tensor_scalar(flag8[:, c * 512:(c + 1) * 512], bank[c][:, :], 0.0, float(NEG8),
                                                   ALU.is_equal, ALU.mult)
                step(last)
                nc.vector.tensor_tensor(adjw, adjw, flagw[:, None, :].to_broadcast([P, T, N // 4]), ALU.bitwise_or)

            @block.tensor
            def _(pe):
                def project(t):
                    pe.wait_ge(xt_copied, t + 1)
                    if t >= 2:
                        pe.wait_ge(v_copied, t - 1)
                    for k in range(KD):
                        nc.tensor.matmul(bank[2 + t % 2][:, :], xnT[:, k, t * P:(t + 1) * P], wseq_sb[:, k, :],
                                         start=(k == 0), stop=(k == KD - 1))
                    for k in range(KD):
                        last = nc.tensor.matmul(bank[4][:, t * 2 * H:(t + 1) * 2 * H], xnT[:, k, t * P:(t + 1) * P],
                                                wa[:, k, :], start=(k == 0), stop=(k == KD - 1))
                    last.then_inc(seq_in_psum, 1)

                pe.wait_ge(consts_loaded, 48)
                pe.wait_ge(wseq_loaded, 16)
                for t in range(T):
                    pe.wait_ge(xn_ready, t + 1)
                    if t >= 2:
                        pe.wait_ge(xt_copied, t - 1)
                    for k in range(KD):
                        last = nc.tensor.transpose(bank[t % 2][:, k * P:(k + 1) * P], x_sb[:, t, k * P:(k + 1) * P], ident)
                    last.then_inc(xt_in_psum, 1)
                    if t == 1:
                        pe.wait_ge(wa_ready, 1)
                    if t >= 1:
                        project(t - 1)
                project(T - 1)
                pe.wait_ge(s_copied, 1)
                for c in range(4):
                    if c >= 2:
                        pe.wait_ge(s1t_copied, c - 1)
                    for q in range(4):
                        last = nc.tensor.transpose(bank[c % 2][0:H, q * P:(q + 1) * P], s_nat[:, 4 * c + q, 0:H], ident)
                    last.then_inc(s1t_in_psum, 1)
                pe.wait_ge(s1t_copied, 4)
                pe.wait_ge(ones_ready, 1)
                pe.wait_ge(adj_cast, T)
                for c in range(4):
                    for j in range(T):
                        last = nc.tensor.matmul(bank[c][:, :], ones16, adj8[:, j, c * 512:(c + 1) * 512],
                                                start=(j == 0), stop=(j == T - 1))
                    last.then_inc(deg_in_psum, 1)

        PAIRS = H // 2
        v_staged = [sem("v_staged_even"), sem("v_staged_odd")]
        s1_staged = [sem("s1_staged_lo"), sem("s1_staged_hi")]
        dve_compared, act_compared, and_step = sem("dve_compared"), sem("act_compared"), sem("and_step")
        m_ready, unit_in_psum, sums_ready, sums_free = sem("m_ready"), sem("unit_in_psum"), sem("sums_ready"), sem("sums_free")
        act_passed, pe_passed = sem("act_passed"), sem("pe_passed")
        bias_copied, scaled_step = sem("bias_copied"), sem("scaled_step")
        GROUPS = [(0, 3), (3, 3), (6, 2)]
        GROUP_OF = [(g, i - GROUPS[g][0]) for i in range(IT) for g in [min(i // 3, 2)]]

        with nc.Block() as block:
            @block.sync
            def _(sp):
                def stage_v(p, b):
                    sp.dma_start(vs[:, b, :, :], vb[:, 2 * p + b, :, :]).then_inc(v_staged[b], 16)

                def stage_s1(p, k):
                    sp.dma_start(s1b[:, k % 2, :],
                                 s1_dram[bass.ds(2 * p + k // 2, 1), (k % 2) * IC:(k % 2 + 1) * IC].to_broadcast([P, IC])
                                 ).then_inc(s1_staged[k % 2], 16)

                for b in range(2):
                    stage_s1(0, b)
                    stage_v(0, b)
                stage_order = [(2, 0), (3, 0), (0, 1), (1, 1)]

                def body(p, last):
                    for k, (nk, dp) in enumerate(stage_order):
                        if not (last and dp):
                            sp.wait_ge(dve_compared, 4 * p + k + 1)
                            sp.wait_ge(act_compared, 4 * p + k + 1)
                            stage_s1(p + dp, nk)
                        if k % 2 and not last:
                            sp.wait_ge(unit_in_psum, 4 * p + k + 1)
                            stage_v(p + 1, k // 2)

                with sp.Fori(0, PAIRS - 1) as p:
                    body(p, False)
                body(PAIRS - 1, True)

            def stage_bias(act, p, b):
                nc.scalar.copy(bias_now[:, b, :], step_bias[:, 2 * p + b, :]).then_inc(bias_copied, 1)

            @block.scalar
            def _(act):
                def compare(p, k):
                    b = k // 2 % 2
                    if k % 2 == 0:
                        stage_bias(act, p, k // 2)
                        act.wait_ge(bias_copied, 2 * p + k // 2 + 1)
                    act.wait_ge(s1_staged[k % 2], 32 * p + 16 * (k // 2 + 1))
                    act.sem_inc(act_passed, 1)
                    for j in range(DVE_J, T):
                        last = nc.scalar.activation(m8[:, k % 2, j, :], s1b[:, k % 2, :], ACT.Sigmoid,
                                                    bias=bias_now[:, b, j:j + 1], scale=STEEP, saturate=False)
                    last.then_inc(act_compared, 1)

                def body(p, last):
                    for k in range(4):
                        if last and k >= 2:
                            continue
                        act.wait_ge(unit_in_psum, 4 * p + k + 1)
                        compare(p + (k + 2) // 4, (k + 2) % 4)

                compare(0, 0)
                compare(0, 1)
                with act.Fori(0, PAIRS - 1) as p:
                    body(p, False)
                body(PAIRS - 1, True)

            @block.vector
            def _(dve):
                def compare(p, k):
                    dve.wait_ge(s1_staged[k % 2], 32 * p + 16 * (k // 2 + 1))
                    for j in range(DVE_J):
                        last = nc.vector.tensor_scalar(mu8[:, k % 2, j, :], s1b[:, k % 2, :],
                                                       neg_s2[:, 2 * p + k // 2, j:j + 1], float(ONE8), ALU.is_gt, ALU.mult)
                    last.then_inc(dve_compared, 1)

                def mask(p, k):
                    cols = slice((k % 2) * IC // 4, (k % 2 + 1) * IC // 4)
                    dve.wait_ge(dve_compared, 4 * p + k + 1)
                    nc.vector.tensor_tensor(mw[:, k % 2, 0:DVE_J, :], mw[:, k % 2, 0:DVE_J, :], adjw[:, 0:DVE_J, cols],
                                            ALU.bitwise_and)
                    dve.wait_ge(act_compared, 4 * p + k + 1)
                    nc.vector.tensor_tensor(mw[:, k % 2, DVE_J:, :], mw[:, k % 2, DVE_J:, :], adjw[:, DVE_J:, cols],
                                            ALU.bitwise_and).then_inc(m_ready, 1)

                def collect(p, k):
                    dve.wait_ge(sums_free, 4 * p + k + 1)
                    for g, (t0, n) in enumerate(GROUPS):
                        last = nc.vector.reduce_sum(
                            sums[:, k % 2, t0:t0 + n, :],
                            bank[3 * (k % 2) + g][:, 0:n * WV].rearrange("p (t s c) -> p t c s", t=n, s=2), AX.X)
                    last.then_inc(sums_ready, 1)

                def body(p, last):
                    for k in range(4):
                        dve.wait_ge(unit_in_psum, 4 * p + k + 1)
                        more = not (last and k >= 2)
                        if more:
                            compare(p + (k + 2) // 4, (k + 2) % 4)
                        collect(p, k)
                        if more:
                            mask(p + (k + 2) // 4, (k + 2) % 4)

                for k in range(2):
                    compare(0, k)
                    mask(0, k)
                with dve.Fori(0, PAIRS - 1) as p:
                    body(p, False)
                body(PAIRS - 1, True)

            @block.gpsimd
            def _(pool):
                pool.sem_inc(sums_free, 2)
                with pool.Fori(0, PAIRS) as p:
                    for k in range(4):
                        h = 2 * p + k // 2
                        tiles = slice((k % 2) * IT, (k % 2 + 1) * IT)
                        pool.wait_ge(sums_ready, 4 * p + k + 1)
                        for c in range(2):
                            last = nc.gpsimd.tensor_tensor(
                                scaled[:, k % 2, :, c * W1:(c + 1) * W1], sums[:, k % 2, :, c * W1:(c + 1) * W1],
                                coef[:, h, tiles, c:c + 1].to_broadcast([P, IT, W1]), ALU.mult)
                        last.then_inc(scaled_step, 1)
                        pool.wait_ge(scaled_step, 4 * p + k + 1)
                        nc.gpsimd.tensor_tensor(hid[:, tiles, h, :], scaled[:, k % 2, :, 0:W1],
                                                scaled[:, k % 2, :, W1:], ALU.add).then_inc(sums_free, 1)

            @block.tensor
            def _(pe):
                with pe.Fori(0, PAIRS) as p:
                    for k in range(4):
                        b = k // 2
                        if k % 2 == 0:
                            pe.wait_ge(v_staged[b], 16 * p + 16)
                        pe.wait_ge(m_ready, 4 * p + k + 1)
                        pe.sem_inc(pe_passed, 1)
                        for i in range(IT):
                            g, slot = GROUP_OF[i]
                            o = bank[3 * (k % 2) + g][:, slot * WV:(slot + 1) * WV]
                            od = o.rearrange("p (s c) -> p s c", s=2)[:, :, W1:WD]
                            for j in range(T):
                                last = nc.tensor.matmul(o, m8[:, k % 2, j, i * P:(i + 1) * P], vs[:, b, j, :],
                                                        start=(j == 0), stop=(j == T - 1))
                                for ja in range(T if j == 0 else 0):
                                    nc.tensor.matmul(
                                        od, adj8[:, ja, (k % 2) * IC + i * P:(k % 2) * IC + (i + 1) * P],
                                        vs[:, b, ja, :].rearrange("p (s c) -> p s c", s=2)[:, :, W1:WD],
                                        start=False, stop=False, skip_group_check=True)
                        last.then_inc(unit_in_psum, 1)

        O_UP, O_DOWN, O_W1, O_W2, O_GATE, O_XT2 = 0, 8192, 16384, 20480, 24576, 24608
        O_WO, O_FC1, O_FC2, O_BUF = 41728, 43776, 44800, 45824
        up_sb = at(O_UP, 8192).rearrange("p (k f) -> p k f", k=KD)
        down_sb = at(O_DOWN, 8192).rearrange("p (f n) -> p f n", f=FS)
        w1_sb = at(O_W1, 4096).rearrange("p (e k i) -> p e k i", e=E, k=KL)
        w2_sb = at(O_W2, 4096).rearrange("p (e k l) -> p e k l", e=E, k=KI)
        gate_sb = at(O_GATE, KD * E).rearrange("p (k e) -> p k e", k=KD)
        xt2 = at(O_XT2, 8192).rearrange("p (k n) -> p k n", k=KD)
        x1 = at(O_HID, T * H * W1).rearrange("p (t c) -> p t c", t=T)[:, :, 0:D]
        wo_sb = at(O_WO, 2048).rearrange("p (k n) -> p k n", k=KD)
        lat_sb = at(O_WO, 1024).rearrange("p (l n) -> p l n", l=KL)
        comb_sb = at(O_WO + 1024, 1024).rearrange("p (l n) -> p l n", l=KL)
        fc1_sb = at(O_FC1, 1024).rearrange("p (k l) -> p k l", k=KD)
        fc2_sb = at(O_FC2, 1024).rearrange("p (k n) -> p k n", k=KL)
        top[0] = O_BUF
        work = small(4096)
        hn = work[:, 0:1024].rearrange("p (b c) -> p b c", b=2)
        hT = work[:, 1024:2048].rearrange("p (b k n) -> p b k n", b=2, k=KD)
        xr = work[:, 2048:3072].rearrange("p (b c) -> p b c", b=2)
        low = work[:, 3072:4096].rearrange("p (b c) -> p b c", b=2)
        relu_sb = work[:, 0:1024].rearrange("p (b c) -> p b c", b=2)
        act2_sb = work[:, 1024:2048].rearrange("p (b c) -> p b c", b=2)
        wrow = work[:, 2048:3072].rearrange("p (b c) -> p b c", b=2)
        o_sb = work[:, 3072:4096].rearrange("p (b c) -> p b c", b=2)
        ident2 = small(P)
        bout_sb = small(D)
        corr_sb = small(E)
        lower_sb = small(E * E)
        rden = small(2 * H).rearrange("p (b h) -> p b h", b=2)
        stat62 = small(2 * 6).rearrange("p (b c) -> p b c", b=2)
        mv2 = small(T * 2).rearrange("p (t c) -> p t c", t=T)
        std2, rstd2 = small(T), small(T)
        score = small(T * E).rearrange("p (t e) -> p t e", t=T)
        sfc = small(T * E).rearrange("p (t e) -> p t e", t=T)
        chosen = small(T * E).rearrange("p (t e) -> p t e", t=T)
        wT = small(512)[0:E, :]
        gsum, ga, gb, gkeep, wsum = (small(2 * T) for _ in range(5))
        xn2 = small(1024).rearrange("p (b c) -> p b c", b=2)
        pairs = work[:, 0:512].rearrange("p (t e f) -> p t e f", t=T, e=E)
        cnt = [work[:, 512 + 128 * i:640 + 128 * i].rearrange("p (t e) -> p t e", t=T) for i in range(4)]

        c2_loaded, wo_loaded, up_loaded, down_loaded, w12_loaded = (sem(n) for n in (
            "c2_loaded", "wo_loaded", "up_loaded", "down_loaded", "w12_loaded"))
        fc_loaded = sem("fc_loaded")
        xr_loaded = [sem("xr_loaded0"), sem("xr_loaded1")]
        ident_ready = sem("ident_ready")
        hn_ready, ht_in_psum, ht_copied, y_in_psum, y_copied = (sem(n) for n in (
            "hn_ready", "ht_in_psum", "ht_copied", "y_in_psum", "y_copied"))
        low_ready, e_ready, low_free, x1_ready, var2_ready, std2_ready, xn2_ready = (sem(n) for n in (
            "low_ready", "e_ready", "low_free", "x1_ready", "var2_ready", "std2_ready", "xn2_ready"))
        xt2_in_psum, xt2_copied, gate_in_psum, score_ready = (sem(n) for n in (
            "xt2_in_psum", "xt2_copied", "gate_in_psum", "score_ready"))
        w_ready, wt_in_psum, wt_copied, w_stored, d2 = (sem(n) for n in (
            "w_ready", "wt_in_psum", "wt_copied", "w_stored", "dve_step2"))

        with nc.Block() as block:
            @block.sync
            def _(sp):
                sp.dma_start(wo_sb, w_out.rearrange("(k p) n -> p k n", p=P)).then_inc(wo_loaded, 16)
                sp.dma_start(bout_sb, b_out[None, :].to_broadcast([P, D])).then_inc(c2_loaded, 16)
                sp.dma_start(corr_sb, corr[None, :].to_broadcast([P, E])).then_inc(c2_loaded, 16)
                sp.dma_start(lower_sb, lower_in[None, :].to_broadcast([P, E * E])).then_inc(c2_loaded, 16)
                sp.dma_start(ident2, ident_in[:, :]).then_inc(c2_loaded, 16)
                sp.dma_start(gate_sb, gateT.rearrange("(k p) e -> p k e", p=P)).then_inc(c2_loaded, 16)
                for t in range(T):
                    if t >= 2:
                        sp.wait_ge(x1_ready, t - 1)
                    sp.dma_start(xr[:, t % 2, :], x[t * P:(t + 1) * P, :]).then_inc(xr_loaded[t % 2], 16)
                for c in range(4):
                    sp.wait_ge(wt_copied, c + 1)
                    sp.dma_start(w_dram[:, c * 512:(c + 1) * 512], wT).then_inc(w_stored, 16)
                    sp.wait_ge(w_stored, 16 * (c + 1))

            @block.scalar
            def _(act):
                act.dma_start(fc1_sb, fc1T.rearrange("(k p) l -> p k l", p=P)).then_inc(fc_loaded, 16)
                act.dma_start(up_sb, upT.rearrange("(k p) f -> p k f", p=P)).then_inc(up_loaded, 16)
                act.dma_start(down_sb, downT.rearrange("(f p) n -> p f n", p=P)).then_inc(down_loaded, 16)
                act.dma_start(w1_sb, w1T.rearrange("e (k p) i -> p e k i", p=P)).then_inc(w12_loaded, 16)
                act.dma_start(w2_sb, w2T.rearrange("e (k p) l -> p e k l", p=P)).then_inc(w12_loaded, 16)
                act.dma_start(fc2_sb, fc2T.rearrange("(k p) n -> p k n", p=P)).then_inc(fc_loaded, 16)

                def copy_xt(t):
                    act.wait_ge(xt2_in_psum, t + 1)
                    nc.scalar.copy(xt2[:, :, t * P:(t + 1) * P],
                                   bank[4 + t % 2][:, :].rearrange("p (k n) -> p k n", k=KD)).then_inc(xt2_copied, 1)

                for g in range(4):
                    for t in range(4 * g, 4 * g + 4):
                        act.wait_ge(ht_in_psum, t + 1)
                        nc.scalar.copy(hT[:, t % 2, :, :],
                                       bank[t % 2][:, :].rearrange("p (k n) -> p k n", k=KD)).then_inc(ht_copied, 1)
                        act.wait_ge(low_ready, t + 1)
                        nc.scalar.activation(low[:, t % 2, :], low[:, t % 2, :], ACT.Exp).then_inc(e_ready, 1)
                    act.wait_ge(var2_ready, g + 1)
                    nc.scalar.activation(std2[:, 4 * g:4 * g + 4], std2[:, 4 * g:4 * g + 4], ACT.Sqrt).then_inc(std2_ready, 1)
                    for t in range(4 * g, 4 * g + 4):
                        copy_xt(t)
                act.wait_ge(gate_in_psum, T)
                nc.scalar.activation(score, bank[6][:, 0:T * E].rearrange("p (t e) -> p t e", t=T),
                                     ACT.Sigmoid).then_inc(score_ready, 1)
                for c in range(4):
                    act.wait_ge(wt_in_psum, c + 1)
                    if c:
                        act.wait_ge(w_stored, 16 * c)
                    nc.scalar.copy(wT, bank[c % 2][0:E, :]).then_inc(wt_copied, 1)

            @block.vector
            def _(dve):
                steps = [0]

                def step(ins):
                    steps[0] += 1
                    ins.then_inc(d2, 1)
                    dve.wait_ge(d2, steps[0])

                dve.wait_ge(c2_loaded, 80)

                def normalise(t):
                    if t >= 2:
                        dve.wait_ge(ht_in_psum, t - 1)
                    step(nc.vector.reciprocal(rden[:, t % 2, :], hid[:, t, :, DH]))
                    nc.vector.tensor_tensor(hn[:, t % 2, :].rearrange("p (h d) -> p h d", h=H), hid[:, t, :, 0:DH],
                                            rden[:, t % 2, :].rearrange("p (h o) -> p h o", o=1).to_broadcast([P, H, DH]),
                                            ALU.mult).then_inc(hn_ready, 1)

                normalise(0)
                for g in range(4):
                    for t in range(4 * g, 4 * g + 4):
                        if t + 1 < T:
                            normalise(t + 1)
                        dve.wait_ge(y_in_psum, t + 1)
                        step(nc.vector.tensor_tensor(x1[:, t, :], bank[2 + t % 2][:, :], bout_sb, ALU.add))
                        step(nc.vector.tensor_scalar(low[:, t % 2, :], x1[:, t, :], 0.0, None, ALU.min))
                        dve.sem_inc(low_ready, 1)
                        step(nc.vector.tensor_scalar(x1[:, t, :], x1[:, t, :], 0.0, -1.0, ALU.max, ALU.add))
                        dve.wait_ge(e_ready, t + 1)
                        step(nc.vector.tensor_tensor(x1[:, t, :], x1[:, t, :], low[:, t % 2, :], ALU.add))
                        dve.wait_ge(xr_loaded[t % 2], 16 * (t // 2 + 1))
                        step(nc.vector.tensor_tensor(x1[:, t, :], x1[:, t, :], xr[:, t % 2, :], ALU.add))
                        dve.sem_inc(x1_ready, 1)
                        step(nc.vector.bn_stats(stat62[:, t % 2, :], x1[:, t, :]))
                        step(nc.vector.bn_aggr(mv2[:, t, :], stat62[:, t % 2, :]))
                    nc.vector.tensor_scalar(std2[:, 4 * g:4 * g + 4], mv2[:, 4 * g:4 * g + 4, 1], EPS, None,
                                            ALU.add).then_inc(var2_ready, 1)
                    dve.wait_ge(std2_ready, g + 1)
                    step(nc.vector.reciprocal(rstd2[:, 4 * g:4 * g + 4], std2[:, 4 * g:4 * g + 4]))
                    for t in range(4 * g, 4 * g + 4):
                        if t >= 2:
                            dve.wait_ge(xt2_in_psum, t - 1)
                        nc.vector.tensor_scalar(xn2[:, t % 2, :], x1[:, t, :], mv2[:, t, 0:1], rstd2[:, t:t + 1],
                                                ALU.subtract, ALU.mult).then_inc(xn2_ready, 1)
                dve.wait_ge(score_ready, 1)
                step(nc.vector.tensor_tensor(sfc, score, corr_sb[:, None, :].to_broadcast([P, T, E]), ALU.add))
                s4 = sfc.rearrange("p t (g c) -> p (t g) c", g=2)
                first = True
                for i in range(4):
                    for j in range(i + 1, 4):
                        dst = gsum if first else ga
                        step(nc.vector.tensor_tensor(dst, s4[:, :, i], s4[:, :, j], ALU.add))
                        if not first:
                            step(nc.vector.tensor_tensor(gsum, gsum, ga, ALU.max))
                        first = False
                gv = gsum.rearrange("p (t g) -> p t g", g=2)
                keep = gkeep.rearrange("p (t g) -> p t g", g=2)
                step(nc.vector.tensor_tensor(keep[:, :, 0], gv[:, :, 0], gv[:, :, 1], ALU.is_ge))
                step(nc.vector.tensor_tensor(keep[:, :, 1], gv[:, :, 0], gv[:, :, 1], ALU.is_lt))
                step(nc.vector.tensor_tensor(s4, s4, gkeep.rearrange("p (a o) -> p a o", o=1).to_broadcast([P, 2 * T, 4]),
                                             ALU.mult))
                for half in range(2):
                    other = sfc[:, :, 4 * half:4 * half + 4]
                    mine = sfc.rearrange("p t (e o) -> p t e o", o=1).to_broadcast([P, T, E, 4])
                    oth = other.rearrange("p t (o f) -> p t o f", o=1).to_broadcast([P, T, E, 4])
                    low_h = lower_sb.rearrange("p (o e f) -> p o e f", o=1, e=E)[:, :, :, 4 * half:4 * half + 4].to_broadcast([P, T, E, 4])
                    step(nc.vector.tensor_tensor(pairs, oth, mine, ALU.is_equal))
                    step(nc.vector.tensor_tensor(pairs, pairs, low_h, ALU.mult))
                    step(nc.vector.reduce_sum(cnt[2 * half], pairs, AX.X))
                    step(nc.vector.tensor_tensor(pairs, oth, mine, ALU.is_gt))
                    step(nc.vector.reduce_sum(cnt[2 * half + 1], pairs, AX.X))
                step(nc.vector.tensor_tensor(chosen, cnt[0], cnt[1], ALU.add))
                step(nc.vector.tensor_tensor(chosen, chosen, cnt[2], ALU.add))
                step(nc.vector.tensor_tensor(chosen, chosen, cnt[3], ALU.add))
                step(nc.vector.tensor_scalar(chosen, chosen, 1.5, None, ALU.is_lt))
                step(nc.vector.tensor_tensor(chosen, chosen, score, ALU.mult))
                step(nc.vector.reduce_sum(wsum[:, 0:T], chosen, AX.X))
                step(nc.vector.tensor_scalar(wsum[:, 0:T], wsum[:, 0:T], 1e-20, None, ALU.add))
                step(nc.vector.reciprocal(wsum[:, T:], wsum[:, 0:T]))
                step(nc.vector.tensor_tensor(chosen, chosen,
                                             wsum[:, T:].rearrange("p (t o) -> p t o", o=1).to_broadcast([P, T, E]), ALU.mult))
                dve.sem_inc(w_ready, 1)

            @block.tensor
            def _(pe):
                pe.wait_ge(c2_loaded, 80)
                pe.wait_ge(wo_loaded, 16)

                def transpose_h(t):
                    pe.wait_ge(hn_ready, t + 1)
                    if t >= 2:
                        pe.wait_ge(ht_copied, t - 1)
                    for k in range(KD):
                        last = nc.tensor.transpose(bank[t % 2][:, k * P:(k + 1) * P], hn[:, t % 2, k * P:(k + 1) * P], ident2)
                    last.then_inc(ht_in_psum, 1)

                def project(t):
                    pe.wait_ge(ht_copied, t + 1)
                    if t >= 2:
                        pe.wait_ge(low_ready, t - 1)
                    for k in range(KD):
                        last = nc.tensor.matmul(bank[2 + t % 2][:, :], hT[:, t % 2, k, :], wo_sb[:, k, :],
                                                start=(k == 0), stop=(k == KD - 1))
                    last.then_inc(y_in_psum, 1)

                def normed(t):
                    pe.wait_ge(xn2_ready, t + 1)
                    if t >= 2:
                        pe.wait_ge(xt2_copied, t - 1)
                    for k in range(KD):
                        last = nc.tensor.transpose(bank[4 + t % 2][:, k * P:(k + 1) * P], xn2[:, t % 2, k * P:(k + 1) * P], ident2)
                    last.then_inc(xt2_in_psum, 1)

                def gate(t):
                    pe.wait_ge(xt2_copied, t + 1)
                    for k in range(KD):
                        last = nc.tensor.matmul(bank[6][:, t * E:(t + 1) * E], xt2[:, k, t * P:(t + 1) * P], gate_sb[:, k, :],
                                                start=(k == 0), stop=(k == KD - 1))
                    last.then_inc(gate_in_psum, 1)

                transpose_h(0)
                for g in range(4):
                    for t in range(4 * g, 4 * g + 4):
                        if t + 1 < T:
                            transpose_h(t + 1)
                        project(t)
                    for t in range(4 * g, 4 * g + 4):
                        normed(t)
                        if t >= 1:
                            gate(t - 1)
                gate(T - 1)
                pe.wait_ge(w_ready, 1)
                for c in range(4):
                    if c >= 2:
                        pe.wait_ge(wt_copied, c - 1)
                    for q in range(4):
                        last = nc.tensor.transpose(bank[c % 2][0:E, q * P:(q + 1) * P], chosen[:, 4 * c + q, :], ident2)
                    last.then_inc(wt_in_psum, 1)

        GEN = KL + FS + E * KI
        EXP0 = KL + FS
        up_in_psum, relu_ready, up_free, h_ready, h_used = (sem(n) for n in (
            "up_in_psum", "relu_ready", "up_free", "h_ready", "h_used"))
        wrow_loaded = [sem("wrow_loaded0"), sem("wrow_loaded1")]
        wrow_used, comb_ready, y2_in_psum, o_ready, sq_step = (sem(n) for n in (
            "wrow_used", "comb_ready", "y2_in_psum", "o_ready", "square_step"))
        o_stored = [sem("o_stored0"), sem("o_stored1")]
        ub, cb, ob = bank[0:2], bank[2:4], bank[4:8]

        with nc.Block() as block:
            @block.sync
            def _(sp):
                with sp.Fori(0, NC_) as c:
                    for e in range(E):
                        sp.wait_ge(wrow_used, E * c + e + 1)
                        sp.dma_start(wrow[:, e % 2, :],
                                     w_dram[e:e + 1, bass.ds(c * TC, TC)].to_broadcast([P, TC])
                                     ).then_inc(wrow_loaded[e % 2], 16)
                    for t in range(TT):
                        sp.wait_ge(o_ready, TT * c + TT + t + 1)
                        sp.dma_start(out[bass.ds(c * TC + t * P, P), :], o_sb[:, t % 2, :]).then_inc(o_stored[t % 2], 16)
                for b in range(2):
                    sp.wait_ge(o_stored[b], 16 * (NC_ * TT // 2 + 1))

            @block.scalar
            def _(act):
                with act.Fori(0, NC_) as c:
                    for n in range(GEN):
                        act.wait_ge(up_in_psum, GEN * c + n + 1)
                        if n < KL:
                            nc.scalar.copy(lat_sb[:, n, :], ub[n % 2][:, :]).then_inc(relu_ready, 1)
                        else:
                            act.wait_ge(up_free, (GEN - KL) * c + n - KL + 1)
                            nc.scalar.activation(relu_sb[:, n % 2, :], ub[n % 2][:, :], ACT.Relu).then_inc(relu_ready, 1)
                    act.wait_ge(h_used, (GEN - KL) * (c + 1) + 2)
                    for l in range(KL):
                        nc.scalar.copy(comb_sb[:, l, :], cb[l][:, :]).then_inc(comb_ready, 1)

            @block.vector
            def _(dve):
                dve.sem_inc(up_free, 2)
                dve.sem_inc(wrow_used, 2)
                dve.sem_inc(o_ready, TT)
                with dve.Fori(0, NC_) as c:
                    for n in range(KL, GEN):
                        m = n - KL
                        dve.wait_ge(relu_ready, GEN * c + n + 1)
                        dve.wait_ge(h_used, (GEN - KL) * c + m + 1)
                        if n < EXP0:
                            ins = nc.vector.tensor_tensor(act2_sb[:, n % 2, :], relu_sb[:, n % 2, :], relu_sb[:, n % 2, :], ALU.mult)
                            ins.then_inc(h_ready, 1)
                            dve.wait_ge(h_ready, (GEN - KL) * c + m + 1)
                            dve.sem_inc(up_free, 1)
                        else:
                            e, q = divmod(n - EXP0, KI)
                            if q == 0:
                                dve.wait_ge(wrow_loaded[e % 2], 16 * (E // 2) * c + 16 * (e // 2 + 1))
                            nc.vector.tensor_tensor(act2_sb[:, n % 2, :], relu_sb[:, n % 2, :], wrow[:, e % 2, :],
                                                    ALU.mult).then_inc(sq_step, 1)
                            dve.wait_ge(sq_step, E * KI * c + n - EXP0 + 1)
                            nc.vector.tensor_tensor(act2_sb[:, n % 2, :], act2_sb[:, n % 2, :], relu_sb[:, n % 2, :],
                                                    ALU.mult).then_inc(h_ready, 1)
                            dve.wait_ge(h_ready, (GEN - KL) * c + m + 1)
                            dve.sem_inc(up_free, 1)
                            if q == KI - 1:
                                dve.sem_inc(wrow_used, 1)
                    for t in range(TT):
                        dve.wait_ge(y2_in_psum, TT * c + t + 1)
                        dve.wait_ge(o_stored[t % 2], 16 * (TT // 2) * c + 16 * (t // 2 + 1))
                        nc.vector.tensor_tensor(o_sb[:, t % 2, :], ob[t][:, :], x1[:, TT * c + t, :], ALU.add).then_inc(o_ready, 1)

            @block.gpsimd
            def _(pool):
                for b in range(2):
                    pool.sem_inc(o_stored[b], 16)

            @block.tensor
            def _(pe):
                pe.sem_inc(h_used, 2)
                pe.wait_ge(up_loaded, 16)
                pe.wait_ge(down_loaded, 16)
                pe.wait_ge(w12_loaded, 32)
                pe.wait_ge(fc_loaded, 32)
                with pe.Fori(0, NC_) as c:
                    def rhs_x(k):
                        return xt2[:, k, bass.ds(c * TC, TC)]

                    def up(n):
                        if n >= 2:
                            pe.wait_ge(relu_ready, GEN * c + n - 1)
                        if n < KL:
                            parts = [(fc1_sb[:, k, n * P:(n + 1) * P], rhs_x(k)) for k in range(KD)]
                        elif n < EXP0:
                            f = n - KL
                            parts = [(up_sb[:, k, f * P:(f + 1) * P], rhs_x(k)) for k in range(KD)]
                        else:
                            e, q = divmod(n - EXP0, KI)
                            parts = [(w1_sb[:, e, k, q * P:(q + 1) * P], lat_sb[:, k, :]) for k in range(KL)]
                        for i, (lhs, rhs) in enumerate(parts):
                            last = nc.tensor.matmul(ub[n % 2][:, :], lhs, rhs, start=(i == 0), stop=(i == len(parts) - 1))
                        last.then_inc(up_in_psum, 1)

                    def down(n):
                        m = n - KL
                        pe.wait_ge(h_ready, (GEN - KL) * c + m + 1)
                        if n < EXP0:
                            if m == 0:
                                pe.wait_ge(o_ready, TT * c + TT)
                            for t in range(TT):
                                last = nc.tensor.matmul(ob[t][:, :], act2_sb[:, n % 2, t * P:(t + 1) * P], down_sb[:, m, :],
                                                        start=(m == 0), stop=False)
                        else:
                            e, q = divmod(n - EXP0, KI)
                            for l in range(KL):
                                last = nc.tensor.matmul(cb[l][:, :], w2_sb[:, e, q, l * P:(l + 1) * P], act2_sb[:, n % 2, :],
                                                        start=(n == EXP0), stop=(n == GEN - 1))
                        last.then_inc(h_used, 1)

                    up(0)
                    up(1)
                    up(2)
                    for n in range(KL, GEN):
                        if n + 1 < GEN:
                            up(n + 1)
                        down(n)
                    pe.wait_ge(comb_ready, KL * c + KL)
                    for t in range(TT):
                        for l in range(KL):
                            last = nc.tensor.matmul(ob[t][:, :], comb_sb[:, l, t * P:(t + 1) * P], fc2_sb[:, l, :],
                                                    start=False, stop=(l == KL - 1))
                        last.then_inc(y2_in_psum, 1)


_INS = ["x", "adjT", "w_seq", "a1", "a2", "w_out", "b_out", "gateT", "corr", "w1T", "w2T", "fc1T", "fc2T", "upT",
        "downT", "ident", "lower"]


def kernel(**inputs):
    import numpy as np
    import concourse.bacc as bacc
    from concourse.bass_utils import run_bass_kernel_spmd

    g = {k: np.asarray(v) for k, v in inputs.items()}
    data = {
        "x": g["x"],
        "adjT": g["adj"].T,
        "w_seq": g["L0_gnn_W_seq"],
        "a1": g["L0_gnn_a1"],
        "a2": g["L0_gnn_a2"],
        "w_out": g["L0_gnn_W_out"],
        "b_out": g["L0_gnn_b_out"],
        "gateT": g["L0_ffn_gate"].T,
        "corr": g["L0_ffn_corr_bias"],
        "w1T": g["L0_ffn_w1"].transpose(0, 2, 1),
        "w2T": g["L0_ffn_w2"].transpose(0, 2, 1),
        "fc1T": g["L0_ffn_fc1_w"].T,
        "fc2T": g["L0_ffn_fc2_w"].T,
        "upT": g["L0_ffn_up_w"].T,
        "downT": g["L0_ffn_down_w"].T,
        "ident": np.eye(P, dtype=np.float32),
        "lower": np.tril(np.ones((E, E), np.float32), -1).reshape(-1),
    }
    nc = bacc.Bacc("TRN2", target_bir_lowering=False, num_devices=1)
    arrays, args = {}, []
    for name in _INS:
        a = np.ascontiguousarray(data[name])
        arrays[f"in_{name}"] = a
        args.append(nc.dram_tensor(f"in_{name}", a.shape, mybir.dt.from_np(a.dtype), kind="ExternalInput").ap())
    args.append(nc.dram_tensor("out_0", (N, D), f32, kind="ExternalOutput").ap())
    build(nc, *args)
    r = run_bass_kernel_spmd(nc, [arrays], core_ids=[0])
    return r.results[0]["out_0"]
```

```python
from contextlib import ExitStack

import concourse.bass as bass
from concourse import mybir

f32 = mybir.dt.float32
f16 = mybir.dt.float16
f8 = mybir.dt.float8e4
f32r = mybir.dt.float32r
u8 = mybir.dt.uint8
u32 = mybir.dt.uint32
ALU = mybir.AluOpType
ACT = mybir.ActivationFunctionType
AX = mybir.AxisListType

P = 128
N = 2048
D = 512
H = 16
DH = D // H
T = N // P
KD = D // P
W1 = DH + 1
WD = 2 * W1
WV = 2 * WD
IC = 1024
IT = IC // P
NIC = N // IC
MB = 4
UNITS = H * NIC
DVE_J = 7
E, LAT, INTER, SH = 8, 256, 256, 2048
TC = 512
NC_ = N // TC
TT = TC // P
KL, KI, FS = LAT // P, INTER // P, SH // P
EPS = 1e-5
ALPHA = 0.2
STEEP = 2.0 ** 60
ONE8, NEG8 = 56, 184
VTOP = 2.0 ** 14


def build(nc, x, adjT, w_seq, a1, a2, w_out, b_out, gateT, corr, w1T, w2T, fc1T, fc2T, upT, downT,
          ident_in, lower_in, out):
    s1_dram = nc.dram_tensor("s1_rows", (H, N), f32, kind="Internal").ap()
    x1_dram = nc.dram_tensor("x1_rows", (N, D), f32, kind="Internal").ap()
    w_dram = nc.dram_tensor("expert_weight_rows", (E, N), f32, kind="Internal").ap()
    ctx = ExitStack()
    with ctx:
        def sem(name):
            return ctx.enter_context(nc.semaphore(name))

        bank = [ctx.enter_context(nc.psum_tensor(f"bank{i}", [P, 512], f32)) for i in range(8)]

        SB0 = -(-nc.sbuf_base // 32) * 32

        def place(name, off, shape, dt=f32):
            return nc.alloc_sbuf_tensor_at(name, [P] + shape, dt, offset=SB0 + 4 * off)[:]

        WORDS = (nc.sbuf_usable_end - SB0) // 4
        O_ARENA = T * H * W1
        hid_t = place("hid", 0, [O_ARENA])
        arena = place("arena", O_ARENA, [WORDS - O_ARENA])

        def at(off, words, dt=f32):
            v = arena[:, off - O_ARENA:off - O_ARENA + words]
            return v if dt == f32 else v.bitcast(dt)

        O_ADJ, O_V, O_M, O_VS, O_VT, O_S1B, O_SUM = O_ARENA, 16640, 24832, 41216, 43328, 44384, 46432
        O_SMALL = O_SUM + 4 * IT * WD
        adj8 = at(O_ADJ, 8192, f8).rearrange("p (j i) -> p j i", j=T)
        adjw = at(O_ADJ, 8192, u32).rearrange("p (j i) -> p j i", j=T)
        x_sb = at(O_M, 8192).rearrange("p (t d) -> p t d", t=T)
        xnT = at(O_M + 8192, 8192).rearrange("p (k n) -> p k n", k=KD)
        m8 = at(O_M, 16384, f8).rearrange("p (b j i) -> p b j i", b=MB, j=T)
        mu8 = at(O_M, 16384, u8).rearrange("p (b j i) -> p b j i", b=MB, j=T)
        mw = at(O_M, 16384, u32).rearrange("p (b j i) -> p b j i", b=MB, j=T)
        adj_in = hid_t[:, 0:8192].rearrange("p (b i) -> p b i", b=4)
        hid = hid_t.rearrange("p (t h c) -> p t h c", t=T, h=H)
        v_sb = at(O_V, T * D).rearrange("p (t d) -> p t d", t=T)
        vs = at(O_VS, 2112, f16).rearrange("p (b j c) -> p b j c", b=2, j=T)
        wa_tmp = at(O_VS, KD * D).rearrange("p (a c) -> p a c", c=DH)
        vtmp = at(O_VT, 1056).rearrange("p (j c) -> p j c", j=T)
        s1b = at(O_S1B, 2048).rearrange("p (b i) -> p b i", b=NIC)
        wseq_sb = at(O_S1B, 2048).rearrange("p (k n) -> p k n", k=KD)
        sums = at(O_SUM, 2 * IT * WD).rearrange("p (b t c) -> p b t c", b=2, t=IT)
        scaled = at(O_SUM + 2 * IT * WD, 2 * IT * WD).rearrange("p (b t c) -> p b t c", b=2, t=IT)
        s1T = at(O_SUM, N)[0:H, :]
        top = [O_SMALL]

        def small(words, dt=f32):
            top[0] += words
            assert top[0] <= WORDS
            return at(top[0] - words, words, dt)

        ident = small(P)
        ones16 = small(P // 2, f16)
        flag8 = small(N // 4, u8)
        flagw = flag8.bitcast(u32)
        s_nat = small(T * 2 * H).rearrange("p (t s) -> p t s", t=T)
        bval = small(T * H).rearrange("p (t h) -> p t h", t=T)
        nval = small(T * H).rearrange("p (t h) -> p t h", t=T)
        zval = small(T * H).rearrange("p (t h) -> p t h", t=T)
        zneg = small(T * H).rearrange("p (t h) -> p t h", t=T)
        neg_s2 = small(H * T).rearrange("p (h t) -> p h t", h=H)
        step_bias = small(H * T).rearrange("p (h t) -> p h t", h=H)
        bias_now = small(2 * T).rearrange("p (b t) -> p b t", b=2)
        coef = small(H * T * 2).rearrange("p (h t c) -> p h t c", h=H, t=T)
        wa = small(KD * 2 * H).rearrange("p (k s) -> p k s", k=KD)
        a_sb = small(2 * DH).rearrange("p (s d) -> p s d", s=2)
        stat6 = small(T * 6).rearrange("p (t c) -> p t c", t=T)
        mv = small(T * 2).rearrange("p (t c) -> p t c", t=T)
        std = small(T)
        rstd = small(T)
        vmx = small(T)
        tops = small(H + 1)
        topr = small(H + 1)
        gfac = small(4)

        x_loaded = [sem(f"x_loaded{g}") for g in range(4)]
        adj_loaded = [sem(f"adj_loaded{g}") for g in range(4)]
        consts_loaded, wseq_loaded = sem("consts_loaded"), sem("wseq_loaded")
        dve_step, act_step, pool_step = sem("dve_step"), sem("act_step"), sem("pool_step")
        wa_ready, var_ready, std_ready, xn_ready = sem("wa_ready"), sem("var_ready"), sem("std_ready"), sem("xn_ready")
        xt_in_psum, xt_copied, seq_in_psum, v_copied = sem("xt_in_psum"), sem("xt_copied"), sem("seq_in_psum"), sem("v_copied")
        s_in_psum = sem("s_in_psum")
        s_copied, s1t_in_psum, s1t_copied, s1_stored = sem("s_copied"), sem("s1t_in_psum"), sem("s1t_copied"), sem("s1_stored")
        tops_ready, topr_ready, expin_ready, exp_ready = sem("tops_ready"), sem("topr_ready"), sem("expin_ready"), sem("exp_ready")
        ones_ready, adj_cast, deg_in_psum = sem("ones_ready"), sem("adj_cast"), sem("deg_in_psum")

        with nc.Block() as block:
            @block.sync
            def _(sp):
                for g in range(4):
                    sp.dma_start(x_sb[:, 4 * g:4 * g + 4, :],
                                 x[512 * g:512 * g + 512, :].rearrange("(t p) d -> p t d", p=P)
                                 ).then_inc(x_loaded[g], 16)
                for g in range(4):
                    sp.wait_ge(x_loaded[g], 16)
                for n in range(T):
                    if n >= 4:
                        sp.wait_ge(adj_cast, n - 3)
                    sp.dma_start(adj_in[:, n % 4, :], adjT[n * P:(n + 1) * P, :]).then_inc(adj_loaded[n % 4], 16)
                sp.wait_ge(s1t_copied, 4)
                sp.dma_start(s1_dram[:, :], s1T).then_inc(s1_stored, 16)
                sp.wait_ge(s1_stored, 16)

            @block.scalar
            def _(act):
                act.dma_start(wseq_sb, w_seq.rearrange("(k p) n -> p k n", p=P)).then_inc(wseq_loaded, 16)
                act.dma_start(a_sb[:, 0, :], a1[None, :].to_broadcast([P, DH])).then_inc(consts_loaded, 16)
                act.dma_start(a_sb[:, 1, :], a2[None, :].to_broadcast([P, DH])).then_inc(consts_loaded, 16)
                act.dma_start(ident, ident_in[:, :]).then_inc(consts_loaded, 16)

                def copy_v(t):
                    act.wait_ge(seq_in_psum, t + 1)
                    nc.scalar.copy(v_sb[:, t, :], bank[2 + t % 2][:, :]).then_inc(v_copied, 1)

                def root(g):
                    act.wait_ge(var_ready, g + 1)
                    nc.scalar.activation(std[:, 4 * g:4 * g + 4], std[:, 4 * g:4 * g + 4], ACT.Sqrt).then_inc(std_ready, 1)

                root(0)
                for g in range(4):
                    for t in range(4 * g, 4 * g + 4):
                        if t % 4 == 2 and g < 3:
                            root(g + 1)
                        act.wait_ge(xt_in_psum, t + 1)
                        nc.scalar.copy(xnT[:, :, t * P:(t + 1) * P],
                                       bank[t % 2][:, :].rearrange("p (k n) -> p k n", k=KD)).then_inc(xt_copied, 1)
                        if t >= 1:
                            copy_v(t - 1)
                copy_v(T - 1)
                for c in range(4):
                    act.wait_ge(s1t_in_psum, c + 1)
                    nc.scalar.copy(s1T[:, c * 512:(c + 1) * 512], bank[c % 2][0:H, :]).then_inc(s1t_copied, 1)
                act.wait_ge(expin_ready, 1)
                nc.scalar.activation(coef.rearrange("p h t c -> p t h c")[:, :, :, 0], zval, ACT.Exp)
                nc.scalar.activation(coef.rearrange("p h t c -> p t h c")[:, :, :, 1], zneg, ACT.Exp)
                nc.scalar.activation(bval, nval, ACT.Exp).then_inc(act_step, 1)
                act.wait_ge(act_step, 1)
                nc.scalar.activation(nval, nval, ACT.Exp, scale=ALPHA).then_inc(exp_ready, 1)

            @block.gpsimd
            def _(pool):
                nc.gpsimd.memset(ones16, 1.0).then_inc(ones_ready, 1)
                pool.wait_ge(tops_ready, 1)
                nc.gpsimd.partition_all_reduce(topr, tops, P, bass.bass_isa.ReduceOp.max).then_inc(topr_ready, 1)

            @block.vector
            def _(dve):
                steps = [0]

                def step(ins):
                    steps[0] += 1
                    ins.then_inc(dve_step, 1)
                    dve.wait_ge(dve_step, steps[0])

                def layer_norm(g):
                    dve.wait_ge(x_loaded[g], 16)
                    tiles = range(4 * g, 4 * g + 4)
                    for t in tiles:
                        last = nc.vector.bn_stats(stat6[:, t, :], x_sb[:, t, :])
                    step(last)
                    for t in tiles:
                        last = nc.vector.bn_aggr(mv[:, t, :], stat6[:, t, :])
                    step(last)
                    nc.vector.tensor_scalar(std[:, 4 * g:4 * g + 4], mv[:, 4 * g:4 * g + 4, 1], EPS, None,
                                            ALU.add).then_inc(var_ready, 1)
                    dve.wait_ge(std_ready, g + 1)
                    step(nc.vector.reciprocal(rstd[:, 4 * g:4 * g + 4], std[:, 4 * g:4 * g + 4]))
                    for t in tiles:
                        nc.vector.tensor_scalar(x_sb[:, t, :], x_sb[:, t, :], mv[:, t, 0:1], rstd[:, t:t + 1],
                                                ALU.subtract, ALU.mult).then_inc(xn_ready, 1)

                def cast_adjacency(t):
                    dve.wait_ge(adj_loaded[t % 4], 16 * (t // 4 + 1))
                    nc.vector.tensor_scalar(adj8[:, t, :], adj_in[:, t % 4, :], -1.0, None, ALU.mult,
                                            saturate=False).then_inc(adj_cast, 1)

                def largest_v(t):
                    dve.wait_ge(v_copied, t + 1)
                    return nc.vector.reduce_max(vmx[:, t:t + 1], v_sb[:, t, :], AX.X, apply_absolute_value=True)

                layer_norm(0)
                dve.wait_ge(wseq_loaded, 16)
                dve.wait_ge(consts_loaded, 48)
                for s in range(2):
                    step(nc.vector.tensor_tensor(wa_tmp, wseq_sb.rearrange("p k (h d) -> p (k h) d", d=DH),
                                                 a_sb[:, s:s + 1, :].to_broadcast([P, KD * H, DH]), ALU.mult))
                    step(nc.vector.reduce_sum(wa[:, :, s * H:(s + 1) * H],
                                              wa_tmp.rearrange("p (k h) d -> p k h d", k=KD), AX.X))
                dve.sem_inc(wa_ready, 1)
                for g in range(1, 4):
                    layer_norm(g)
                for t in range(T):
                    cast_adjacency(t)
                    if t % 2:
                        largest_v(t // 2)
                for t in range(T // 2, T):
                    last = largest_v(t)
                step(last)
                nc.vector.reduce_max(tops[:, H:H + 1], vmx, AX.X)
                dve.wait_ge(s_in_psum, T)
                nc.vector.tensor_copy(s_nat, bank[4][:, :].rearrange("p (t s) -> p t s", t=T)).then_inc(s_copied, 1)
                dve.wait_ge(s_copied, 1)
                nc.vector.reduce_max(tops[:, 0:H], s_nat[:, :, H:].rearrange("p t h -> p h t"), AX.X).then_inc(tops_ready, 1)
                nc.vector.tensor_scalar(neg_s2, s_nat[:, :, H:].rearrange("p t h -> p h t"), -1.0, None, ALU.mult)
                nc.vector.tensor_scalar(step_bias, s_nat[:, :, H:].rearrange("p t h -> p h t"), STEEP, None, ALU.mult)
                dve.wait_ge(topr_ready, 1)
                topb = topr[:, None, 0:H].to_broadcast([P, T, H])
                step(nc.vector.tensor_tensor(zval, s_nat[:, :, 0:H], topb, ALU.add))
                step(nc.vector.tensor_scalar(zneg, zval, -(1 - ALPHA), 0.0, ALU.mult, ALU.min))
                step(nc.vector.tensor_scalar(zval, zval, 1 - ALPHA, 0.0, ALU.mult, ALU.min))
                nc.vector.tensor_tensor(nval, s_nat[:, :, H:], topb, ALU.subtract).then_inc(expin_ready, 1)
                step(nc.vector.tensor_scalar(gfac[:, 0:1], topr[:, H:H + 1], 1.0, None, ALU.max))
                step(nc.vector.reciprocal(gfac[:, 1:2], gfac[:, 0:1]))
                step(nc.vector.tensor_scalar(gfac[:, 2:3], gfac[:, 1:2], VTOP, None, ALU.mult))
                step(nc.vector.tensor_scalar(gfac[:, 3:4], gfac[:, 1:2], -VTOP, None, ALU.mult))
                dve.wait_ge(exp_ready, 1)
                step(nc.vector.tensor_scalar(bval, bval, gfac[:, 2:3], None, ALU.mult))
                nc.vector.tensor_scalar(nval, nval, gfac[:, 3:4], None, ALU.mult)

                for c in range(4):
                    words = slice(c * P, (c + 1) * P)
                    dve.wait_ge(deg_in_psum, c + 1)
                    step(nc.vector.tensor_scalar(flag8[:, c * 512:(c + 1) * 512], bank[c][:, :], 0.0, float(NEG8),
                                                 ALU.is_equal, ALU.mult))
                    nc.vector.tensor_tensor(adjw[:, :, words], adjw[:, :, words],
                                            flagw[:, None, words].to_broadcast([P, T, P]), ALU.bitwise_or)

            @block.tensor
            def _(pe):
                def project(t):
                    pe.wait_ge(xt_copied, t + 1)
                    if t >= 2:
                        pe.wait_ge(v_copied, t - 1)
                    for k in range(KD):
                        last = nc.tensor.matmul(bank[2 + t % 2][:, :], xnT[:, k, t * P:(t + 1) * P], wseq_sb[:, k, :],
                                                start=(k == 0), stop=(k == KD - 1))
                    last.then_inc(seq_in_psum, 1)

                def scores(t):
                    for k in range(KD):
                        last = nc.tensor.matmul(bank[4][:, t * 2 * H:(t + 1) * 2 * H], xnT[:, k, t * P:(t + 1) * P],
                                                wa[:, k, :], start=(k == 0), stop=(k == KD - 1))
                    last.then_inc(s_in_psum, 1)

                pe.wait_ge(consts_loaded, 48)
                pe.wait_ge(wseq_loaded, 16)
                for t in range(T):
                    pe.wait_ge(xn_ready, t + 1)
                    if t >= 2:
                        pe.wait_ge(xt_copied, t - 1)
                    for k in range(KD):
                        last = nc.tensor.transpose(bank[t % 2][:, k * P:(k + 1) * P], x_sb[:, t, k * P:(k + 1) * P], ident)
                    last.then_inc(xt_in_psum, 1)
                    if t >= 1:
                        project(t - 1)
                    if t == 4:
                        pe.wait_ge(wa_ready, 1)
                    if t >= 4:
                        scores(t - 4)
                project(T - 1)
                for t in range(T - 4, T):
                    scores(t)
                pe.wait_ge(s_copied, 1)
                for c in range(4):
                    if c >= 2:
                        pe.wait_ge(s1t_copied, c - 1)
                    for q in range(4):
                        last = nc.tensor.transpose(bank[c % 2][0:H, q * P:(q + 1) * P], s_nat[:, 4 * c + q, 0:H], ident)
                    last.then_inc(s1t_in_psum, 1)
                pe.wait_ge(s1t_copied, 4)
                pe.wait_ge(ones_ready, 1)
                pe.wait_ge(adj_cast, T)
                for c in range(4):
                    for j in range(T):
                        last = nc.tensor.matmul(bank[c][:, :], ones16, adj8[:, j, c * 512:(c + 1) * 512],
                                                start=(j == 0), stop=(j == T - 1))
                    last.then_inc(deg_in_psum, 1)

        x1 = hid_t.rearrange("p (t c) -> p t c", t=T)[:, :, 0:D]
        up_sb = place("up_sb", 8448, [KD, SH])
        down_sb = place("down_sb", 16640, [FS, D])
        xhl = [place("xt_high", 41216, [KD, N], f32r), place("xt_low", 33024, [KD, N], f32r)]
        wo_sb = place("wo_sb", 24832, [KD, D])
        xr = place("xr", 26880, [2, D])
        ident2 = place("ident2", 27904, [P])
        bout_sb = place("bout_sb", 28032, [D])
        corr_sb = place("corr_sb", 28544, [E])
        gate_sb = place("gate_sb", 28552, [KD, E])
        lower_sb = place("lower_sb", 28584, [E, E])
        hn = place("hn", 28928, [2, D])
        hT = place("hT", 29952, [2, KD, P])
        pos = place("pos", 30976, [2, D])
        neg = place("neg", 32000, [2, D])
        top[0] = 49408

        def small_at(name, shape, dt=f32):
            words = 1
            for s in shape:
                words *= s
            top[0] += -(-words // 8) * 8
            assert top[0] <= WORDS
            return place(name, top[0] - -(-words // 8) * 8, shape, dt)

        xn2 = small_at("xn2", [2, D])
        ones_row = small_at("ones_row", [P])
        gate_hl = small_at("gate_hl", [2, KD, E], f32r)
        rden = small_at("rden", [T, H])
        stat62 = small_at("stat62", [2, 6])
        mv2 = small_at("mv2", [T, 2])
        std2, rstd2 = small_at("std2", [T]), small_at("rstd2", [T])
        enx = small_at("enx", [T, E])
        score, sfc, chosen = (small_at(n, [4, E]) for n in ("score", "sfc", "chosen"))
        gtop, gtry, gkeep = (small_at(n, [4, 2]) for n in ("gtop", "gtry", "gkeep"))
        pairs, larger = small_at("pairs", [4, E, E]), small_at("larger", [4, E, E])
        wsum = small_at("wsum", [2, 4])
        w_all = small_at("w_all", [T, E])
        wT = small_at("wT", [512])[0:E, :]
        GT = 4
        LAGX, LAGG = 5, 8

        c2_loaded, wo_loaded, up_loaded, down_loaded = (sem(n) for n in ("c2_loaded", "wo_loaded", "up_loaded", "down_loaded"))
        xr_loaded = [sem("xr_loaded0"), sem("xr_loaded1")]
        rden_ready, hn_ready, ht_in_psum, ht_copied, y_in_psum, pos_ready, neg_step, e_ready = (sem(n) for n in (
            "rden_ready", "hn_ready", "ht_in_psum", "ht_copied", "y_in_psum", "pos_ready", "neg_step", "e_ready"))
        x1_ready, var2_ready, std2_ready, xn2_ready, xt2_in_psum, xth_copied, xtl_ready, gate_ready = (sem(n) for n in (
            "x1_ready", "var2_ready", "std2_ready", "xn2_ready", "xt2_in_psum", "xth_copied", "xtl_ready", "gate_ready"))
        gate_in_psum, enx_ready, w_ready, wt_in_psum, wt_copied, w_stored, d2, x1_stored, ones2_ready = (sem(n) for n in (
            "gate_in_psum", "enx_ready", "w_ready", "wt_in_psum", "wt_copied", "w_stored", "dve_step2",
            "x1_stored", "ones2_ready"))

        PAIRS = H // 2
        prod_ready, hi_copied, lo_ready, vtmp_free = sem("prod_ready"), sem("hi_copied"), sem("lo_ready"), sem("vtmp_free")
        s1_staged = [sem("s1_staged_lo"), sem("s1_staged_hi")]
        dve_compared, act_compared, own_masked = sem("dve_compared"), sem("act_compared"), sem("own_masked")
        m_ready, unit_in_psum, sums_ready, sums_free = sem("m_ready"), sem("unit_in_psum"), sem("sums_ready"), sem("sums_free")
        act_passed, pe_passed = sem("act_passed"), sem("pe_passed")
        bias_copied, scaled_step = sem("bias_copied"), sem("scaled_step")
        GROUPS = [(0, 3), (3, 3), (6, 2)]
        GROUP_OF = [(g, i - GROUPS[g][0]) for i in range(IT) for g in [min(i // 3, 2)]]

        with nc.Block() as block:
            @block.sync
            def _(sp):
                def stage_s1(p, k):
                    sp.dma_start(s1b[:, k % 2, :],
                                 s1_dram[bass.ds(2 * p + k // 2, 1), (k % 2) * IC:(k % 2 + 1) * IC].to_broadcast([P, IC])
                                 ).then_inc(s1_staged[k % 2], 16)

                def body(p, last):
                    for k in range(4):
                        if not (last and k >= 2):
                            sp.wait_ge(dve_compared, 4 * p + k + 1)
                            sp.wait_ge(act_compared, 4 * p + k + 1)
                            stage_s1(p + (k + 2) // 4, (k + 2) % 4)

                stage_s1(0, 0)
                stage_s1(0, 1)
                with sp.Fori(0, PAIRS - 1) as p:
                    body(p, False)
                body(PAIRS - 1, True)
                sp.wait_ge(unit_in_psum, UNITS - 3)
                sp.dma_start(wo_sb, w_out.rearrange("(k p) n -> p k n", p=P)).then_inc(wo_loaded, 16)
                sp.dma_start(ident2, ident_in[:, :]).then_inc(c2_loaded, 16)
                sp.dma_start(bout_sb[0:1, :], b_out[None, :]).then_inc(c2_loaded, 16)
                sp.dma_start(corr_sb, corr[None, :].to_broadcast([P, E])).then_inc(c2_loaded, 16)
                sp.dma_start(lower_sb.rearrange("p e f -> p (e f)"), lower_in[None, :].to_broadcast([P, E * E])).then_inc(c2_loaded, 16)
                sp.dma_start(gate_sb, gateT.rearrange("(k p) e -> p k e", p=P)).then_inc(c2_loaded, 16)
                for t in range(2):
                    sp.dma_start(xr[:, t, :], x[t * P:(t + 1) * P, :]).then_inc(xr_loaded[t], 16)

            @block.scalar
            def _(act):
                def compare(p, k):
                    b = k // 2
                    if k % 2 == 0:
                        nc.scalar.copy(bias_now[:, b, :], step_bias[:, 2 * p + b, :]).then_inc(bias_copied, 1)
                        act.wait_ge(bias_copied, 2 * p + b + 1)
                    act.wait_ge(s1_staged[k % 2], 32 * p + 16 * (k // 2 + 1))
                    act.sem_inc(act_passed, 1)
                    for j in range(DVE_J, T):
                        last = nc.scalar.activation(m8[:, k, j, :], s1b[:, k % 2, :], ACT.Sigmoid,
                                                    bias=bias_now[:, b, j:j + 1], scale=STEEP, saturate=False)
                    last.then_inc(act_compared, 1)

                def split_high(p, b):
                    act.wait_ge(prod_ready, 2 * p + b + 1)
                    nc.scalar.copy(vs[:, b, :, 0:WD], vtmp).then_inc(hi_copied, 1)

                def body(p, last):
                    for k in range(4):
                        act.wait_ge(unit_in_psum, 4 * p + k + 1)
                        if not last:
                            if k % 2:
                                split_high(p + 1, k // 2)
                            compare(p + 1, k)

                split_high(0, 0)
                compare(0, 0)
                split_high(0, 1)
                for k in range(1, 4):
                    compare(0, k)
                with act.Fori(0, PAIRS - 1) as p:
                    body(p, False)

            @block.vector
            def _(dve):
                def compare(p, k):
                    dve.wait_ge(s1_staged[k % 2], 32 * p + 16 * (k // 2 + 1))
                    for j in range(DVE_J):
                        last = nc.vector.tensor_scalar(mu8[:, k, j, :], s1b[:, k % 2, :],
                                                       neg_s2[:, 2 * p + k // 2, j:j + 1], float(ONE8), ALU.is_gt, ALU.mult)
                    last.then_inc(dve_compared, 1)

                def mask_own(p, k):
                    cols = slice((k % 2) * IC // 4, (k % 2 + 1) * IC // 4)
                    dve.wait_ge(dve_compared, 4 * p + k + 1)
                    nc.vector.tensor_tensor(mw[:, k, 0:DVE_J, :], mw[:, k, 0:DVE_J, :], adjw[:, 0:DVE_J, cols],
                                            ALU.bitwise_and).then_inc(own_masked, 1)

                def mask_acts(p, k):
                    cols = slice((k % 2) * IC // 4, (k % 2 + 1) * IC // 4)
                    dve.wait_ge(act_compared, 4 * p + k + 1)
                    dve.wait_ge(own_masked, 4 * p + k + 1)
                    nc.vector.tensor_tensor(mw[:, k, DVE_J:, :], mw[:, k, DVE_J:, :], adjw[:, DVE_J:, cols],
                                            ALU.bitwise_and).then_inc(m_ready, 1)

                def collect(p, k):
                    dve.wait_ge(sums_free, 4 * p + k + 1)
                    for g, (t0, n) in enumerate(GROUPS):
                        last = nc.vector.reduce_sum(
                            sums[:, k % 2, t0:t0 + n, :],
                            bank[3 * (k % 2) + g][:, 0:n * WV].rearrange("p (t s c) -> p t c s", t=n, s=2), AX.X)
                    last.then_inc(sums_ready, 1)

                def body(p, last):
                    for k in range(4):
                        dve.wait_ge(unit_in_psum, 4 * p + k + 1)
                        collect(p, k)
                        if not last:
                            compare(p + 1, k)
                            mask_own(p + 1, k)
                        if k == 0:
                            mask_acts(p, 3)
                        elif not last:
                            mask_acts(p + 1, k - 1)

                dve.sem_inc(sums_ready, 2)
                for k in range(4):
                    compare(0, k)
                    mask_own(0, k)
                    if k:
                        mask_acts(0, k - 1)
                with dve.Fori(0, PAIRS - 1) as p:
                    body(p, False)
                body(PAIRS - 1, True)

            @block.gpsimd
            def _(pool):
                def build(p, b):
                    h = 2 * p + b
                    pool.wait_ge(vtmp_free, 2 * p + b + 1)
                    vh = v_sb.rearrange("p t (h d) -> p t h d", h=H)[:, :, h, :]
                    for c, val in enumerate((bval, nval)):
                        nc.gpsimd.tensor_tensor(vtmp[:, :, c * W1:c * W1 + DH], vh,
                                                val[:, :, bass.ds(h, 1)].to_broadcast([P, T, DH]), ALU.mult)
                        last = nc.gpsimd.tensor_copy(vtmp[:, :, c * W1 + DH:(c + 1) * W1], val[:, :, bass.ds(h, 1)])
                    last.then_inc(prod_ready, 1)
                    pool.wait_ge(prod_ready, 2 * p + b + 1)
                    pool.wait_ge(hi_copied, 2 * p + b + 1)
                    nc.gpsimd.tensor_tensor(vs[:, b, :, WD:], vtmp, vs[:, b, :, 0:WD], ALU.subtract).then_inc(lo_ready, 1)
                    pool.wait_ge(lo_ready, 2 * p + b + 1)
                    pool.sem_inc(vtmp_free, 1)

                def combine(p, k):
                    h = 2 * p + k // 2
                    tiles = slice((k % 2) * IT, (k % 2 + 1) * IT)
                    pool.wait_ge(sums_ready, 4 * p + k + 3)
                    for c in range(2):
                        last = nc.gpsimd.tensor_tensor(
                            scaled[:, k % 2, :, c * W1:(c + 1) * W1], sums[:, k % 2, :, c * W1:(c + 1) * W1],
                            coef[:, h, tiles, c:c + 1].to_broadcast([P, IT, W1]), ALU.mult)
                    last.then_inc(scaled_step, 1)
                    pool.wait_ge(scaled_step, 4 * p + k + 1)
                    nc.gpsimd.tensor_tensor(hid[:, tiles, h, :], scaled[:, k % 2, :, 0:W1],
                                            scaled[:, k % 2, :, W1:], ALU.add).then_inc(sums_free, 1)

                def body(p, last):
                    for k in range(4):
                        if k % 2 and not last:
                            pool.wait_ge(unit_in_psum, 4 * p + k + 1)
                            build(p + 1, k // 2)
                        combine(p, k)

                pool.sem_inc(sums_free, 2)
                pool.sem_inc(vtmp_free, 1)
                build(0, 0)
                build(0, 1)
                with pool.Fori(0, PAIRS - 1) as p:
                    body(p, False)
                body(PAIRS - 1, True)

            @block.tensor
            def _(pe):
                with pe.Fori(0, PAIRS) as p:
                    for k in range(4):
                        b = k // 2
                        if k % 2 == 0:
                            pe.wait_ge(lo_ready, 2 * p + b + 1)
                        pe.wait_ge(sums_ready, 4 * p + k + 1)
                        pe.wait_ge(m_ready, 4 * p + k + 1)
                        pe.sem_inc(pe_passed, 1)
                        for i in range(IT):
                            g, slot = GROUP_OF[i]
                            o = bank[3 * (k % 2) + g][:, slot * WV:(slot + 1) * WV]
                            od = o.rearrange("p (s c) -> p s c", s=2)[:, :, W1:WD]
                            for j in range(T):
                                last = nc.tensor.matmul(o, m8[:, k, j, i * P:(i + 1) * P], vs[:, b, j, :],
                                                        start=(j == 0), stop=(j == T - 1))
                                for ja in range(T if j == 0 else 0):
                                    nc.tensor.matmul(
                                        od, adj8[:, ja, (k % 2) * IC + i * P:(k % 2) * IC + (i + 1) * P],
                                        vs[:, b, ja, :].rearrange("p (s c) -> p s c", s=2)[:, :, W1:WD],
                                        start=False, stop=False, skip_group_check=True)
                        last.then_inc(unit_in_psum, 1)

        with nc.Block() as block:
            @block.sync
            def _(sp):
                for t in range(2, T):
                    sp.wait_ge(x1_ready, t - 1)
                    sp.dma_start(x1_dram[(t - 2) * P:(t - 1) * P, :], x1[:, t - 2, :]).then_inc(x1_stored, 16)
                    sp.dma_start(xr[:, t % 2, :], x[t * P:(t + 1) * P, :]).then_inc(xr_loaded[t % 2], 16)
                for t in range(T - 2, T):
                    sp.wait_ge(x1_ready, t + 1)
                    sp.dma_start(x1_dram[t * P:(t + 1) * P, :], x1[:, t, :]).then_inc(x1_stored, 16)
                for g in range(4):
                    sp.wait_ge(wt_copied, g + 1)
                    sp.dma_start(w_dram[:, g * 512:(g + 1) * 512], wT).then_inc(w_stored, 16)
                    sp.wait_ge(w_stored, 16 * (g + 1))
                sp.wait_ge(x1_stored, 16 * T)

            @block.scalar
            def _(act):
                act.dma_start(up_sb, upT.rearrange("(k p) f -> p k f", p=P)).then_inc(up_loaded, 16)
                act.dma_start(down_sb, downT.rearrange("(f p) n -> p f n", p=P)).then_inc(down_loaded, 16)

                def copy_h(t):
                    act.wait_ge(ht_in_psum, t + 1)
                    if t >= 2:
                        act.wait_ge(y_in_psum, t - 1)
                    nc.scalar.copy(hT[:, t % 2, :, :],
                                   bank[t % 2][:, :].rearrange("p (k n) -> p k n", k=KD)).then_inc(ht_copied, 1)

                def elu_parts(t):
                    act.wait_ge(y_in_psum, t + 1)
                    if t >= 2:
                        act.wait_ge(x1_ready, t - 1)
                    nc.scalar.activation(neg[:, t % 2, :], bank[2 + t % 2][:, :], ACT.Relu, scale=-1.0).then_inc(neg_step, 1)
                    nc.scalar.activation(pos[:, t % 2, :], bank[2 + t % 2][:, :], ACT.Relu).then_inc(pos_ready, 1)
                    act.wait_ge(neg_step, t + 1)
                    nc.scalar.activation(neg[:, t % 2, :], neg[:, t % 2, :], ACT.Exp, scale=-1.0).then_inc(e_ready, 1)

                def root(g):
                    act.wait_ge(var2_ready, g + 1)
                    nc.scalar.activation(std2[:, GT * g:GT * g + GT], std2[:, GT * g:GT * g + GT], ACT.Sqrt).then_inc(std2_ready, 1)

                def high_of_xt(t):
                    act.wait_ge(xt2_in_psum, t + 1)
                    nc.scalar.copy(xhl[0][:, :, t * P:(t + 1) * P],
                                   bank[4 + t % 2][:, :].rearrange("p (k n) -> p k n", k=KD)).then_inc(xth_copied, 1)

                def exp_gate(g):
                    act.wait_ge(gate_in_psum, GT * (g + 1))
                    nc.scalar.activation(enx[:, GT * g:GT * g + GT, :],
                                         bank[6 + g % 2][:, 0:GT * E].rearrange("p (t e) -> p t e", t=GT),
                                         ACT.Exp, scale=-1.0).then_inc(enx_ready, 1)

                def copy_w(g):
                    act.wait_ge(wt_in_psum, g + 1)
                    if g:
                        act.wait_ge(w_stored, 16 * g)
                    nc.scalar.copy(wT, bank[0][0:E, :]).then_inc(wt_copied, 1)

                copy_h(0)
                for t in range(T + LAGG + 1):
                    if t % GT == 0 and 1 <= t // GT <= 4:
                        root(t // GT - 1)
                    if t + 1 < T:
                        copy_h(t + 1)
                    if t < T:
                        elu_parts(t)
                    if 0 <= t - LAGX - 1 < T:
                        high_of_xt(t - LAGX - 1)
                    if t - LAGG >= GT - 1 and (t - LAGG) % GT == GT - 1:
                        exp_gate((t - LAGG) // GT)
                for g in range(4):
                    copy_w(g)

            @block.gpsimd
            def _(pool):
                nc.gpsimd.memset(ones_row, 1.0).then_inc(ones2_ready, 1)
                pool.wait_ge(rden_ready, 1)

                def normalise(t):
                    if t >= 2:
                        pool.wait_ge(ht_in_psum, t - 1)
                    nc.gpsimd.tensor_tensor(hn[:, t % 2, :].rearrange("p (h d) -> p h d", h=H), hid[:, t, :, 0:DH],
                                            rden[:, t, :].rearrange("p (h o) -> p h o", o=1).to_broadcast([P, H, DH]),
                                            ALU.mult).then_inc(hn_ready, 1)

                for t in range(T):
                    normalise(t)

            @block.vector
            def _(dve):
                steps = [0]

                def step(ins):
                    steps[0] += 1
                    ins.then_inc(d2, 1)
                    dve.wait_ge(d2, steps[0])

                nc.vector.reciprocal(rden, hid[:, :, :, DH]).then_inc(rden_ready, 1)
                dve.wait_ge(c2_loaded, 80)
                step(nc.vector.tensor_copy(gate_hl[:, 0, :, :], gate_sb))
                nc.vector.tensor_tensor(gate_hl[:, 1, :, :], gate_sb, gate_hl[:, 0, :, :].bitcast(f32),
                                        ALU.subtract).then_inc(gate_ready, 1)

                def residual(t):
                    dve.wait_ge(xr_loaded[t % 2], 16 * (t // 2 + 1))
                    dve.wait_ge(pos_ready, t + 1)
                    dve.wait_ge(hn_ready, t + 1)
                    step(nc.vector.scalar_tensor_tensor(out=x1[:, t, :], in0=xr[:, t % 2, :], scalar=-1.0,
                                                        in1=pos[:, t % 2, :], op0=ALU.add, op1=ALU.add))
                    dve.wait_ge(e_ready, t + 1)
                    nc.vector.tensor_tensor(x1[:, t, :], x1[:, t, :], neg[:, t % 2, :], ALU.add).then_inc(x1_ready, 1)
                    dve.wait_ge(x1_ready, t + 1)
                    step(nc.vector.bn_stats(stat62[:, t % 2, :], x1[:, t, :]))
                    step(nc.vector.bn_aggr(mv2[:, t, :], stat62[:, t % 2, :]))

                def norm(t):
                    if t >= 2:
                        dve.wait_ge(xt2_in_psum, t - 1)
                    nc.vector.tensor_scalar(xn2[:, t % 2, :], x1[:, t, :], mv2[:, t, 0:1], rstd2[:, t:t + 1],
                                            ALU.subtract, ALU.mult).then_inc(xn2_ready, 1)

                def low_of_xt(t):
                    dve.wait_ge(xth_copied, t + 1)
                    cols = slice(t * P, (t + 1) * P)
                    nc.vector.tensor_tensor(xhl[1][:, :, cols], bank[4 + t % 2][:, :].rearrange("p (k n) -> p k n", k=KD),
                                            xhl[0][:, :, cols].bitcast(f32), ALU.subtract).then_inc(xtl_ready, 1)

                def route(g):
                    tt = nc.vector.tensor_tensor
                    dve.wait_ge(enx_ready, g + 1)
                    now = enx[:, GT * g:GT * g + GT, :]
                    step(nc.vector.tensor_scalar(now, now, 1.0, None, ALU.add))
                    step(nc.vector.reciprocal(score, now))
                    step(tt(sfc, score, corr_sb[:, None, :].to_broadcast([P, GT, E]), ALU.add))
                    s4 = sfc.rearrange("p t (g c) -> p t g c", g=2)
                    for n, (i, j) in enumerate((i, j) for i in range(4) for j in range(i + 1, 4)):
                        step(tt(gtry if n else gtop, s4[:, :, :, i], s4[:, :, :, j], ALU.add))
                        if n:
                            step(tt(gtop, gtop, gtry, ALU.max))
                    step(tt(gkeep[:, :, 0], gtop[:, :, 0], gtop[:, :, 1], ALU.is_ge))
                    step(tt(gkeep[:, :, 1], gtop[:, :, 0], gtop[:, :, 1], ALU.is_lt))
                    step(tt(s4, s4, gkeep.rearrange("p t (g o) -> p t g o", o=1).to_broadcast([P, GT, 2, 4]), ALU.mult))
                    mine = sfc.rearrange("p t (e o) -> p t e o", o=1).to_broadcast([P, GT, E, E])
                    other = sfc.rearrange("p t (o f) -> p t o f", o=1).to_broadcast([P, GT, E, E])
                    step(tt(pairs, other, mine, ALU.is_equal))
                    step(tt(pairs, pairs, lower_sb[:, None, :, :].to_broadcast([P, GT, E, E]), ALU.mult))
                    step(tt(larger, other, mine, ALU.is_gt))
                    step(tt(pairs, pairs, larger, ALU.add))
                    step(nc.vector.reduce_sum(chosen, pairs, AX.X))
                    step(nc.vector.tensor_scalar(chosen, chosen, 1.5, None, ALU.is_lt))
                    step(tt(chosen, chosen, score, ALU.mult))
                    step(nc.vector.reduce_sum(wsum[:, 0, :], chosen, AX.X))
                    step(nc.vector.tensor_scalar(wsum[:, 0, :], wsum[:, 0, :], 1e-20, None, ALU.add))
                    step(nc.vector.reciprocal(wsum[:, 1, :], wsum[:, 0, :]))
                    tt(w_all[:, GT * g:GT * g + GT, :], chosen,
                       wsum[:, 1, :].rearrange("p (t o) -> p t o", o=1).to_broadcast([P, GT, E]), ALU.mult).then_inc(w_ready, 1)
                    dve.wait_ge(w_ready, g + 1)

                for t in range(T + LAGG + 2):
                    if t < T:
                        residual(t)
                    if t < T and t % GT == GT - 1:
                        g = t // GT
                        nc.vector.tensor_scalar(std2[:, GT * g:GT * g + GT], mv2[:, GT * g:GT * g + GT, 1], EPS, None,
                                                ALU.add).then_inc(var2_ready, 1)
                    if 0 <= t - LAGX < T:
                        if (t - LAGX) % GT == 0:
                            g = (t - LAGX) // GT
                            dve.wait_ge(std2_ready, g + 1)
                            step(nc.vector.reciprocal(rstd2[:, GT * g:GT * g + GT], std2[:, GT * g:GT * g + GT]))
                        norm(t - LAGX)
                    if 0 <= t - LAGX - 2 < T:
                        low_of_xt(t - LAGX - 2)
                    if t - LAGG - 1 >= GT - 1 and (t - LAGG - 1) % GT == GT - 1:
                        route((t - LAGG - 1) // GT)

            @block.tensor
            def _(pe):
                def transpose_h(t):
                    pe.wait_ge(hn_ready, t + 1)
                    if t >= 2:
                        pe.wait_ge(ht_copied, t - 1)
                    for k in range(KD):
                        last = nc.tensor.transpose(bank[t % 2][:, k * P:(k + 1) * P], hn[:, t % 2, k * P:(k + 1) * P], ident2)
                    last.then_inc(ht_in_psum, 1)

                def project(t):
                    pe.wait_ge(ht_copied, t + 1)
                    if t >= 2:
                        pe.wait_ge(pos_ready, t - 1)
                    nc.tensor.matmul(bank[2 + t % 2][:, :], ones_row[0:1, :], bout_sb[0:1, :], start=True, stop=False)
                    for k in range(KD):
                        last = nc.tensor.matmul(bank[2 + t % 2][:, :], hT[:, t % 2, k, :], wo_sb[:, k, :],
                                                start=False, stop=(k == KD - 1))
                    last.then_inc(y_in_psum, 1)

                def transpose_x(t):
                    pe.wait_ge(xn2_ready, t + 1)
                    if t >= 2:
                        pe.wait_ge(xtl_ready, t - 1)
                    for k in range(KD):
                        last = nc.tensor.transpose(bank[4 + t % 2][:, k * P:(k + 1) * P], xn2[:, t % 2, k * P:(k + 1) * P], ident2)
                    last.then_inc(xt2_in_psum, 1)

                def gate(t):
                    pe.wait_ge(xtl_ready, t + 1)
                    if t % GT == 0 and t >= 2 * GT:
                        pe.wait_ge(enx_ready, t // GT - 1)
                    terms = [(k, a, b) for k in range(KD) for a, b in ((0, 0), (0, 1), (1, 0))]
                    for n, (k, a, b) in enumerate(terms):
                        last = nc.tensor.matmul(bank[6 + t // GT % 2][:, t % GT * E:(t % GT + 1) * E], xhl[a][:, k, t * P:(t + 1) * P],
                                                gate_hl[:, b, k, :], start=(n == 0), stop=(n == len(terms) - 1))
                    last.then_inc(gate_in_psum, 1)

                pe.wait_ge(c2_loaded, 80)
                pe.wait_ge(ones2_ready, 1)
                transpose_h(0)
                pe.wait_ge(wo_loaded, 16)
                pe.wait_ge(gate_ready, 1)
                for t in range(T + LAGG):
                    if t + 1 < T:
                        transpose_h(t + 1)
                    if t < T:
                        project(t)
                    if 0 <= t - LAGX - 1 < T:
                        transpose_x(t - LAGX - 1)
                    if 0 <= t - LAGG < T:
                        gate(t - LAGG)
                for g in range(4):
                    pe.wait_ge(w_ready, g + 1)
                    if g:
                        pe.wait_ge(wt_copied, g)
                    for q in range(GT):
                        last = nc.tensor.transpose(bank[0][0:E, q * P:(q + 1) * P], w_all[:, GT * g + q, :], ident2)
                    last.then_inc(wt_in_psum, 1)

        GEN = KL + FS + E * KI
        EXP0 = KL + FS
        NS = GEN - KL
        EB = 4
        ew = place("expert_weights", 0, [EB, 2, KL * INTER])
        hhl = place("h_parts", 4096, [2, 2, TC], f32r)
        sa = place("up_parts", 6144, [2, 2, KD, P], f32r)
        sb_ = place("down_parts", 24832, [2, 2, D], f32r)
        lhl = place("latent_parts", 26880, [2, KL, TC], f32r)
        comb_sb = place("comb_sb", 28928, [KL, TC])
        relu_sb = place("relu_sb", 29952, [2, TC])
        wrow = place("wrow", 30976, [2, TC])
        fc1_sb = place("fc1_sb", 32000, [KD, LAT])
        fc2_sb = place("fc2_sb", 49408, [KL, D])
        acc = place("acc", 50432, [TT, D])
        rw = place("relu_weighted", 52480, [TC])
        assert 52480 + TC <= WORDS

        cb, ob = bank[2:4], bank[4:8]

        def up_bank(n):
            if n < KL:
                return bank[2 + n]
            if n < EXP0:
                return bank[(n - KL) % 4]
            return (bank[0], bank[1], bank[4], bank[5])[(n - EXP0) % 4]

        fc_loaded, lat_ready, sp_passed = sem("fc_loaded"), sem("lat_ready"), sem("sp_passed")
        ew_loaded = [sem(f"ew_loaded{i}") for i in range(EB)]
        wrow_loaded = [sem("wrow_loaded0"), sem("wrow_loaded1")]
        a_high, a_ready, b_high, b_ready, up_in_psum, relu_ready, sq_ready, w_scaled, h_high, h_ready, down_done = (
            sem(n) for n in ("a_high", "a_ready", "b_high", "b_ready", "up_in_psum", "relu_ready", "sq_ready", "w_scaled",
                             "h_high", "h_ready", "down_done"))
        expert_used, comb_ready, y2_in_psum, acc_done = (sem(n) for n in ("expert_used", "comb_ready", "y2_in_psum", "acc_done"))
        x1_loaded = [sem(f"x1_loaded{t}") for t in range(TT)]
        stored = [sem(f"stored{t}") for t in range(TT)]

        def a_source(n):
            if n < KL:
                return fc1_sb[:, :, n * P:(n + 1) * P]
            if n < EXP0:
                return up_sb[:, :, (n - KL) * P:(n - KL + 1) * P]
            e, q = divmod(n - EXP0, KI)
            return ew[:, e % EB, 0, :].rearrange("p (k i) -> p k i", k=KL)[:, :, q * P:(q + 1) * P]

        def b_source(n):
            if n < EXP0:
                return down_sb[:, n - KL, :]
            e, q = divmod(n - EXP0, KI)
            return ew[:, e % EB, 1, q * LAT:(q + 1) * LAT]

        def expert_loaded(eng, c, n):
            if n >= EXP0 and (n - EXP0) % KI == 0:
                e = (n - EXP0) // KI
                eng.wait_ge(ew_loaded[e % EB], 32 * (E // EB) * c + 32 * (e // EB + 1))

        with nc.Block() as block:
            @block.sync
            def _(sp):
                with sp.Fori(0, NC_) as c:
                    for t in range(TT):
                        sp.wait_ge(stored[t], 16 * c + 16)
                        sp.sem_inc(sp_passed, 1)
                        sp.dma_start(acc[:, t, :], x1_dram[bass.ds(c * TC + t * P, P), :]).then_inc(x1_loaded[t], 16)
                    for e in range(E):
                        sp.wait_ge(expert_used, E * c + e + 1)
                        sp.dma_start(ew[:, e % EB, 0, :].rearrange("p (k i) -> p k i", k=KL),
                                     w1T[e].rearrange("(k p) i -> p k i", p=P)).then_inc(ew_loaded[e % EB], 16)
                        sp.dma_start(ew[:, e % EB, 1, :].rearrange("p (k l) -> p k l", k=KI),
                                     w2T[e].rearrange("(k p) l -> p k l", p=P)).then_inc(ew_loaded[e % EB], 16)
                        sp.wait_ge(expert_used, E * c + e + 1 + EB - 2)
                        sp.sem_inc(sp_passed, 1)
                        sp.dma_start(wrow[:, e % 2, :],
                                     w_dram[e:e + 1, bass.ds(c * TC, TC)].to_broadcast([P, TC])
                                     ).then_inc(wrow_loaded[e % 2], 16)
                    for t in range(TT):
                        sp.wait_ge(acc_done, 2 * TT * c + 3 * TT + t + 1)
                        sp.sem_inc(sp_passed, 1)
                        sp.dma_start(out[bass.ds(c * TC + t * P, P), :], acc[:, t, :]).then_inc(stored[t], 16)
                for t in range(TT):
                    sp.wait_ge(stored[t], 16 * (NC_ + 1))

            @block.scalar
            def _(act):
                act.dma_start(fc1_sb, fc1T.rearrange("(k p) l -> p k l", p=P)).then_inc(fc_loaded, 16)
                act.dma_start(fc2_sb, fc2T.rearrange("(k p) n -> p k n", p=P)).then_inc(fc_loaded, 16)
                act.wait_ge(fc_loaded, 32)

                def high_a(c, n):
                    expert_loaded(act, c, n)
                    src = a_source(n)
                    nc.scalar.copy(sa[:, n % 2, 0, 0:src.shape[1], :], src).then_inc(a_high, 1)

                high_a(0, 0)
                high_a(0, 1)
                with act.Fori(0, NC_) as c:
                    for n in range(GEN):
                        act.wait_ge(up_in_psum, GEN * c + n + 1)
                        if n < KL:
                            nc.scalar.copy(lhl[:, 0, n, :], up_bank(n)[:, :]).then_inc(relu_ready, 1)
                        else:
                            act.wait_ge(h_ready, NS * c + n - KL + 1)
                            nc.scalar.activation(relu_sb[:, n % 2, :], up_bank(n)[:, :], ACT.Relu).then_inc(relu_ready, 1)
                        high_a(c, (n + 2) % GEN)
                        if n >= KL:
                            m = n - KL
                            act.wait_ge(down_done, NS * c + m + 1)
                            src = b_source(n)
                            nc.scalar.copy(sb_[:, n % 2, 0, 0:src.shape[1]], src).then_inc(b_high, 1)
                            act.wait_ge(sq_ready, NS * c + m + 1)
                            nc.scalar.copy(hhl[:, n % 2, 0, :], relu_sb[:, n % 2, :]).then_inc(h_high, 1)
                    act.wait_ge(down_done, NS * c + NS + 2)
                    for l in range(KL):
                        nc.scalar.copy(comb_sb[:, l, :], cb[l][:, :]).then_inc(comb_ready, 1)

            @block.vector
            def _(dve):
                dve.sem_inc(h_ready, 2)
                dve.sem_inc(expert_used, EB)
                dve.sem_inc(acc_done, 2 * TT)

                def low_a(n, count):
                    dve.wait_ge(a_high, count)
                    src = a_source(n)
                    kk = src.shape[1]
                    nc.vector.tensor_tensor(sa[:, n % 2, 1, 0:kk, :], src, sa[:, n % 2, 0, 0:kk, :].bitcast(f32),
                                            ALU.subtract).then_inc(a_ready, 1)

                low_a(0, 1)
                low_a(1, 2)
                with dve.Fori(0, NC_) as c:
                    for n in range(GEN):
                        m = n - KL
                        r = relu_sb[:, n % 2, :]
                        dve.wait_ge(relu_ready, GEN * c + n + 1)
                        if n < KL:
                            nc.vector.tensor_tensor(lhl[:, 1, n, :], up_bank(n)[:, :], lhl[:, 0, n, :].bitcast(f32),
                                                    ALU.subtract).then_inc(lat_ready, 1)
                        elif n < EXP0:
                            nc.vector.tensor_tensor(r, r, r, ALU.mult).then_inc(sq_ready, 1)
                        else:
                            e, q = divmod(n - EXP0, KI)
                            if q == 0:
                                dve.wait_ge(wrow_loaded[e % 2], 16 * (E // 2) * c + 16 * (e // 2 + 1))
                            nc.vector.tensor_tensor(rw, r, wrow[:, e % 2, :], ALU.mult).then_inc(w_scaled, 1)
                            dve.wait_ge(w_scaled, E * KI * c + n - EXP0 + 1)
                            nc.vector.tensor_tensor(r, r, rw, ALU.mult).then_inc(sq_ready, 1)
                        low_a((n + 2) % GEN, GEN * c + n + 3)
                        if n >= KL:
                            dve.wait_ge(b_high, NS * c + m + 1)
                            src = b_source(n)
                            w = src.shape[1]
                            nc.vector.tensor_tensor(sb_[:, n % 2, 1, 0:w], src, sb_[:, n % 2, 0, 0:w].bitcast(f32),
                                                    ALU.subtract).then_inc(b_ready, 1)
                            dve.wait_ge(h_high, NS * c + m + 1)
                            nc.vector.tensor_tensor(hhl[:, n % 2, 1, :], r, hhl[:, n % 2, 0, :].bitcast(f32),
                                                    ALU.subtract).then_inc(h_ready, 1)
                            if n >= EXP0 and (n - EXP0) % KI == KI - 1:
                                dve.wait_ge(h_ready, NS * c + m + 3)
                                dve.sem_inc(expert_used, 1)
                        if n == EXP0:
                            dve.wait_ge(down_done, NS * c + FS + 2)
                            for t in range(TT):
                                dve.wait_ge(x1_loaded[t], 16 * c + 16)
                                nc.vector.tensor_tensor(acc[:, t, :], ob[t][:, :], acc[:, t, :], ALU.add).then_inc(acc_done, 1)
                    for t in range(TT):
                        dve.wait_ge(y2_in_psum, TT * c + t + 1)
                        dve.wait_ge(acc_done, 2 * TT * c + 2 * TT + t + 1)
                        nc.vector.tensor_tensor(acc[:, t, :], ob[t][:, :], acc[:, t, :], ALU.add).then_inc(acc_done, 1)

            @block.gpsimd
            def _(pool):
                for t in range(TT):
                    pool.sem_inc(stored[t], 16)

            @block.tensor
            def _(pe):
                TERMS = ((0, 0), (0, 1), (1, 0))
                pe.sem_inc(down_done, 2)
                pe.wait_ge(fc_loaded, 32)
                with pe.Fori(0, NC_) as c:
                    def up(n):
                        if n in (KL + 2, KL + 3):
                            pe.wait_ge(lat_ready, KL * c + n - KL - 1)
                        elif n in (EXP0 + 2, EXP0 + 3):
                            pe.wait_ge(acc_done, 2 * TT * c + 2 * TT + n - EXP0 - 1)
                        elif n > KL + 3:
                            pe.wait_ge(relu_ready, GEN * c + n - 3)
                        if n == EXP0:
                            pe.wait_ge(lat_ready, KL * c + KL)
                        pe.wait_ge(a_ready, GEN * c + n + 1)
                        kk = KD if n < EXP0 else KL
                        mm = [(k, a, b) for k in range(kk) for a, b in TERMS]
                        for i, (k, a, b) in enumerate(mm):
                            rhs = xhl[b][:, k, bass.ds(c * TC, TC)] if n < EXP0 else lhl[:, b, k, :]
                            last = nc.tensor.matmul(up_bank(n)[:, :], sa[:, n % 2, a, k, :], rhs,
                                                    start=(i == 0), stop=(i == len(mm) - 1))
                        last.then_inc(up_in_psum, 1)

                    def down(n):
                        m = n - KL
                        if m == 0:
                            pe.wait_ge(acc_done, 2 * TT * c + 2 * TT)
                        pe.wait_ge(h_ready, NS * c + m + 3)
                        if n < EXP0:
                            for t in range(TT):
                                for a, b in TERMS:
                                    last = nc.tensor.matmul(ob[t][:, :], hhl[:, n % 2, a, t * P:(t + 1) * P], sb_[:, n % 2, b, :],
                                                            start=(m == 0 and (a, b) == TERMS[0]),
                                                            stop=(n == EXP0 - 1 and (a, b) == TERMS[-1]))
                        else:
                            for l in range(KL):
                                for a, b in TERMS:
                                    last = nc.tensor.matmul(cb[l][:, :], sb_[:, n % 2, a, l * P:(l + 1) * P], hhl[:, n % 2, b, :],
                                                            start=(n == EXP0 and (a, b) == TERMS[0]),
                                                            stop=(n == GEN - 1 and (a, b) == TERMS[-1]))
                        last.then_inc(down_done, 1)

                    up(0)
                    up(1)
                    for n in range(GEN):
                        if n + 2 < GEN:
                            up(n + 2)
                        if n >= KL:
                            down(n)
                    pe.wait_ge(comb_ready, KL * c + KL)
                    for t in range(TT):
                        for l in range(KL):
                            last = nc.tensor.matmul(ob[t][:, :], comb_sb[:, l, t * P:(t + 1) * P], fc2_sb[:, l, :],
                                                    start=(l == 0), stop=(l == KL - 1))
                        last.then_inc(y2_in_psum, 1)


_INS = ["x", "adjT", "w_seq", "a1", "a2", "w_out", "b_out", "gateT", "corr", "w1T", "w2T", "fc1T", "fc2T", "upT",
        "downT", "ident", "lower"]


def kernel(**inputs):
    import numpy as np
    import concourse.bacc as bacc
    from concourse.bass_utils import run_bass_kernel_spmd

    g = {k: np.asarray(v) for k, v in inputs.items()}
    data = {
        "x": g["x"],
        "adjT": g["adj"].T,
        "w_seq": g["L0_gnn_W_seq"],
        "a1": g["L0_gnn_a1"],
        "a2": g["L0_gnn_a2"],
        "w_out": g["L0_gnn_W_out"],
        "b_out": g["L0_gnn_b_out"],
        "gateT": g["L0_ffn_gate"].T,
        "corr": g["L0_ffn_corr_bias"],
        "w1T": g["L0_ffn_w1"].transpose(0, 2, 1),
        "w2T": g["L0_ffn_w2"].transpose(0, 2, 1),
        "fc1T": g["L0_ffn_fc1_w"].T,
        "fc2T": g["L0_ffn_fc2_w"].T,
        "upT": g["L0_ffn_up_w"].T,
        "downT": g["L0_ffn_down_w"].T,
        "ident": np.eye(P, dtype=np.float32),
        "lower": np.tril(np.ones((E, E), np.float32), -1).reshape(-1),
    }
    nc = bacc.Bacc("TRN2", target_bir_lowering=False, num_devices=1)
    arrays, args = {}, []
    for name in _INS:
        a = np.ascontiguousarray(data[name])
        arrays[f"in_{name}"] = a
        args.append(nc.dram_tensor(f"in_{name}", a.shape, mybir.dt.from_np(a.dtype), kind="ExternalInput").ap())
    args.append(nc.dram_tensor("out_0", (N, D), f32, kind="ExternalOutput").ap())
    build(nc, *args)
    r = run_bass_kernel_spmd(nc, [arrays], core_ids=[0])
    return r.results[0]["out_0"]
```

```python
from contextlib import ExitStack

import concourse.bass as bass
from concourse import mybir

f32 = mybir.dt.float32
f16 = mybir.dt.float16
f8 = mybir.dt.float8e4
f32r = mybir.dt.float32r
u8 = mybir.dt.uint8
u32 = mybir.dt.uint32
ALU = mybir.AluOpType
ACT = mybir.ActivationFunctionType
AX = mybir.AxisListType

P = 128
N = 2048
D = 512
H = 16
DH = D // H
T = N // P
KD = D // P
W1 = DH + 1
WD = 2 * W1
WV = 2 * WD
IC = 1024
IT = IC // P
NIC = N // IC
MB = 4
AB = 3
UNITS = H * NIC
DVE_J = 7
E, LAT, INTER, SH = 8, 256, 256, 2048
TC = 512
NC_ = N // TC
TT = TC // P
KL, KI, FS = LAT // P, INTER // P, SH // P
EPS = 1e-5
ALPHA = 0.2
STEEP = 2.0 ** 60
ONE8, NEG8 = 56, 184
VTOP = 2.0 ** 14


def build(nc, x, adjT, w_seq, a1, a2, w_out, b_out, gateT, corr, w1T, w2T, fc1T, fc2T, upT, downT,
          ident_in, lower_in, out):
    s1_dram = nc.dram_tensor("s1_rows", (H, N), f32, kind="Internal").ap()
    x1_dram = nc.dram_tensor("x1_rows", (N, D), f32, kind="Internal").ap()
    w_dram = nc.dram_tensor("expert_weight_rows", (E, N), f32, kind="Internal").ap()
    ctx = ExitStack()
    with ctx:
        def sem(name):
            return ctx.enter_context(nc.semaphore(name))

        bank = [ctx.enter_context(nc.psum_tensor(f"bank{i}", [P, 512], f32)) for i in range(8)]

        SB0 = -(-nc.sbuf_base // 32) * 32

        def place(name, off, shape, dt=f32):
            return nc.alloc_sbuf_tensor_at(name, [P] + shape, dt, offset=SB0 + 4 * off)[:]

        WORDS = (nc.sbuf_usable_end - SB0) // 4
        O_ARENA = T * H * W1
        hid_t = place("hid", 0, [O_ARENA])
        arena = place("arena", O_ARENA, [WORDS - O_ARENA])

        def at(off, words, dt=f32):
            v = arena[:, off - O_ARENA:off - O_ARENA + words]
            return v if dt == f32 else v.bitcast(dt)

        O_ADJ, O_V, O_M, O_VS, O_VT, O_S1B, O_SUM = O_ARENA, 16640, 24832, 41216, 43328, 44384, 46432
        O_SMALL = O_SUM + 4 * IT * WD
        adj8 = at(O_ADJ, 8192, f8).rearrange("p (j i) -> p j i", j=T)
        adjw = at(O_ADJ, 8192, u32).rearrange("p (j i) -> p j i", j=T)
        x_sb = at(O_M, 8192).rearrange("p (t d) -> p t d", t=T)
        xnT = at(O_M + 8192, 8192).rearrange("p (k n) -> p k n", k=KD)
        m8 = at(O_M, 16384, f8).rearrange("p (b j i) -> p b j i", b=MB, j=T)
        mu8 = at(O_M, 16384, u8).rearrange("p (b j i) -> p b j i", b=MB, j=T)
        mw = at(O_M, 16384, u32).rearrange("p (b j i) -> p b j i", b=MB, j=T)
        adj_in = hid_t[:, 0:AB * N].rearrange("p (b i) -> p b i", b=AB)
        wseq_sb = hid_t[:, AB * N:AB * N + KD * D].rearrange("p (k n) -> p k n", k=KD)
        hid = hid_t.rearrange("p (t h c) -> p t h c", t=T, h=H)
        v_sb = at(O_V, T * D).rearrange("p (t d) -> p t d", t=T)
        vs = at(O_VS, 2112, f16).rearrange("p (b j c) -> p b j c", b=2, j=T)
        wa_tmp = at(O_VS, 2 * KD * D).rearrange("p (s k h d) -> p s k h d", s=2, k=KD, h=H)
        vtmp = at(O_VT, 1056).rearrange("p (j c) -> p j c", j=T)
        s1b = at(O_S1B, 2048).rearrange("p (b i) -> p b i", b=NIC)
        sums = at(O_SUM, 2 * IT * WD).rearrange("p (b t c) -> p b t c", b=2, t=IT)
        scaled = at(O_SUM + 2 * IT * WD, 2 * IT * WD).rearrange("p (b t c) -> p b t c", b=2, t=IT)
        sT = at(O_SUM, N)[0:2 * H, :]
        top = [O_SMALL]

        def small(words, dt=f32):
            top[0] += words
            assert top[0] <= WORDS
            return at(top[0] - words, words, dt)

        ident = small(P)
        ones16 = small(P // 2, f16)
        flag8 = small(N // 4, u8)
        flagw = flag8.bitcast(u32)
        s_nat = small(T * 2 * H).rearrange("p (t s) -> p t s", t=T)
        bval = small(T * H).rearrange("p (t h) -> p t h", t=T)
        nval = small(T * H).rearrange("p (t h) -> p t h", t=T)
        zval = small(T * H).rearrange("p (t h) -> p t h", t=T)
        zneg = small(T * H).rearrange("p (t h) -> p t h", t=T)
        neg_s2 = small(H * T).rearrange("p (h t) -> p h t", h=H)
        step_bias = small(H * T).rearrange("p (h t) -> p h t", h=H)
        bias_now = small(2 * T).rearrange("p (b t) -> p b t", b=2)
        coef = small(H * T * 2).rearrange("p (h t c) -> p h t c", h=H, t=T)
        wa = small(KD * 2 * H).rearrange("p (k s) -> p k s", k=KD)
        a_sb = small(2 * DH).rearrange("p (s d) -> p s d", s=2)
        stat6 = small(T * 6).rearrange("p (t c) -> p t c", t=T)
        mv = small(T * 2).rearrange("p (t c) -> p t c", t=T)
        std = small(T)
        rstd = small(T)
        vmx = small(T)
        tops = small(H + 1)
        topr = small(H + 1)
        gfac = small(4)

        x_loaded = [sem(f"x_loaded{g}") for g in range(4)]
        adj_loaded = [sem(f"adj_loaded{g}") for g in range(AB)]
        consts_loaded, wseq_loaded = sem("consts_loaded"), sem("wseq_loaded")
        dve_step, act_step = sem("dve_step"), sem("act_step")
        wa_ready, var_ready, std_ready, xn_ready = sem("wa_ready"), sem("var_ready"), sem("std_ready"), sem("xn_ready")
        xt_in_psum, xt_copied, seq_in_psum, v_copied = sem("xt_in_psum"), sem("xt_copied"), sem("seq_in_psum"), sem("v_copied")
        s_in_psum = sem("s_in_psum")
        s_copied, st_in_psum, st_copied, s1_stored = sem("s_copied"), sem("st_in_psum"), sem("st_copied"), sem("s1_stored")
        tops_ready, topr_ready, expin_ready, exp_ready = sem("tops_ready"), sem("topr_ready"), sem("expin_ready"), sem("exp_ready")
        s1_staged = [sem("s1_staged_lo"), sem("s1_staged_hi")]
        bn_ready = sem("bn_ready")
        ones_ready, deg_in_psum = sem("ones_ready"), sem("deg_in_psum")
        adj_cast, wa_step = sem("adj_cast"), sem("wa_step")

        SEQ_BANK = [bank[2], bank[3], bank[5], bank[6]]
        DEG_BANK = [bank[0], bank[1], bank[7], bank[6]]

        def setup_loads(sp):
            for g in range(4):
                sp.dma_start(x_sb[:, 4 * g:4 * g + 4, :],
                             x[512 * g:512 * g + 512, :].rearrange("(t p) d -> p t d", p=P)
                             ).then_inc(x_loaded[g], 16)
            for g in range(4):
                sp.wait_ge(x_loaded[g], 16)
            for n in range(T):
                if n >= AB:
                    sp.wait_ge(adj_cast, n - AB + 1)
                sp.dma_start(adj_in[:, n % AB, :], adjT[n * P:(n + 1) * P, :]).then_inc(adj_loaded[n % AB], 16)

        def setup_act(act):
            act.dma_start(ident, ident_in[:, :]).then_inc(consts_loaded, 16)
            act.dma_start(a_sb[:, 0, :], a1[None, :].to_broadcast([P, DH])).then_inc(consts_loaded, 16)
            act.dma_start(a_sb[:, 1, :], a2[None, :].to_broadcast([P, DH])).then_inc(consts_loaded, 16)
            act.dma_start(wseq_sb, w_seq.rearrange("(k p) n -> p k n", p=P)).then_inc(wseq_loaded, 16)

            def copy_xt(g):
                for t in range(4 * g, 4 * g + 4):
                    act.wait_ge(xt_in_psum, t + 1)
                    nc.scalar.copy(xnT[:, :, t * P:(t + 1) * P],
                                   bank[t % 2][:, :].rearrange("p (k n) -> p k n", k=KD)).then_inc(xt_copied, 1)

            def copy_v(*tiles):
                for t in tiles:
                    act.wait_ge(seq_in_psum, t + 1)
                    nc.scalar.copy(v_sb[:, t, :], SEQ_BANK[t % 4][:, :]).then_inc(v_copied, 1)

            def root(g):
                act.wait_ge(var_ready, g + 1)
                nc.scalar.activation(std[:, 4 * g:4 * g + 4], std[:, 4 * g:4 * g + 4], ACT.Sqrt).then_inc(std_ready, 1)

            root(0)
            for g in range(4):
                copy_xt(g)
                if g == 0:
                    root(1)
                copy_v(g)
                if g < 2:
                    root(g + 2)
            for c in range(4):
                act.wait_ge(st_in_psum, c + 1)
                nc.scalar.copy(sT[:, c * 512:(c + 1) * 512], bank[4 + 3 * (c % 2)][0:2 * H, :]).then_inc(st_copied, 1)
            act.wait_ge(st_copied, 4)
            act.dma_start(s1_dram[:, :], sT[0:H, :]).then_inc(s1_stored, 16)
            act.wait_ge(expin_ready, 1)
            nc.scalar.activation(coef.rearrange("p h t c -> p t h c")[:, :, :, 0], zval, ACT.Exp)
            nc.scalar.activation(coef.rearrange("p h t c -> p t h c")[:, :, :, 1], zneg, ACT.Exp)
            nc.scalar.activation(bval, nval, ACT.Exp).then_inc(act_step, 1)
            act.wait_ge(act_step, 1)
            nc.scalar.activation(nval, nval, ACT.Exp, scale=ALPHA).then_inc(exp_ready, 1)
            act.wait_ge(s1_stored, 16)
            for k in range(2):
                act.dma_start(s1b[:, k, :], s1_dram[0:1, k * IC:(k + 1) * IC].to_broadcast([P, IC])).then_inc(s1_staged[k], 16)
            return copy_v

        def setup_pool(pool):
            nc.gpsimd.memset(ones16, 1.0).then_inc(ones_ready, 1)
            pool.wait_ge(wseq_loaded, 16)
            pool.wait_ge(consts_loaded, 48)
            for k in range(2):
                last = nc.gpsimd.tensor_tensor(wa_tmp[:, k].rearrange("p k h d -> p (k h) d"), wseq_sb.rearrange("p k (h d) -> p (k h) d", d=DH),
                                        a_sb[:, k:k + 1, :].to_broadcast([P, KD * H, DH]), ALU.mult)
            last.then_inc(wa_step, 1)
            half = DH // 2
            steps = 1
            rows = wa_tmp.rearrange("p s k h d -> p (s k h) d")
            while half > 1:
                pool.wait_ge(wa_step, steps)
                nc.gpsimd.tensor_tensor(rows[:, :, 0:half], rows[:, :, 0:half], rows[:, :, half:2 * half],
                                        ALU.add).then_inc(wa_step, 1)
                steps += 1
                half //= 2
            pool.wait_ge(wa_step, steps)
            for k in range(2):
                last = nc.gpsimd.tensor_tensor(wa[:, :, k * H:(k + 1) * H], wa_tmp[:, k, :, :, 0], wa_tmp[:, k, :, :, 1], ALU.add)
            last.then_inc(wa_ready, 1)
            for n, cols in enumerate((slice(0, H), slice(H, H + 1))):
                pool.wait_ge(tops_ready, n + 1)
                nc.gpsimd.partition_all_reduce(topr[:, cols], tops[:, cols], P, bass.bass_isa.ReduceOp.max).then_inc(topr_ready, 1)

        def setup_dve(dve):
            steps = [0]

            def step(ins):
                steps[0] += 1
                ins.then_inc(dve_step, 1)
                dve.wait_ge(dve_step, steps[0])

            def layer_norm(g):
                dve.wait_ge(x_loaded[g], 16)
                tiles = range(4 * g, 4 * g + 4)
                for t in tiles:
                    last = nc.vector.bn_stats(stat6[:, t, :], x_sb[:, t, :])
                step(last)
                for t in tiles:
                    last = nc.vector.bn_aggr(mv[:, t, :], stat6[:, t, :])
                step(last)
                nc.vector.tensor_scalar(std[:, 4 * g:4 * g + 4], mv[:, 4 * g:4 * g + 4, 1], EPS, None,
                                        ALU.add).then_inc(var_ready, 1)
                dve.wait_ge(std_ready, g + 1)
                step(nc.vector.reciprocal(rstd[:, 4 * g:4 * g + 4], std[:, 4 * g:4 * g + 4]))
                for t in tiles:
                    nc.vector.tensor_scalar(x_sb[:, t, :], x_sb[:, t, :], mv[:, t, 0:1], rstd[:, t:t + 1],
                                            ALU.subtract, ALU.mult).then_inc(xn_ready, 1)

            def cast_adjacency(*tiles):
                for t in tiles:
                    dve.wait_ge(adj_loaded[t % AB], 16 * (t // AB + 1))
                    nc.vector.tensor_scalar(adj8[:, t, :], adj_in[:, t % AB, :], -1.0, None, ALU.mult,
                                            saturate=False).then_inc(adj_cast, 1)

            def largest_v(*tiles):
                for t in tiles:
                    dve.wait_ge(v_copied, t + 1)
                    last = nc.vector.reduce_max(vmx[:, t:t + 1], v_sb[:, t, :], AX.X, apply_absolute_value=True)
                return last

            for g in range(4):
                layer_norm(g)
            cast_adjacency(0, 1, 2, 3, 4, 5)
            dve.wait_ge(s_in_psum, 1)
            nc.vector.tensor_copy(s_nat, bank[0][:, :].rearrange("p (t s) -> p t s", t=T)).then_inc(s_copied, 1)
            dve.wait_ge(s_copied, 1)
            nc.vector.reduce_max(tops[:, 0:H], s_nat[:, :, H:].rearrange("p t h -> p h t"), AX.X).then_inc(tops_ready, 1)
            nc.vector.tensor_scalar(neg_s2, s_nat[:, :, H:].rearrange("p t h -> p h t"), -1.0, None, ALU.mult)
            nc.vector.tensor_scalar(step_bias, s_nat[:, :, H:].rearrange("p t h -> p h t"), STEEP, None, ALU.mult)
            dve.wait_ge(topr_ready, 1)
            topb = topr[:, None, 0:H].to_broadcast([P, T, H])
            step(nc.vector.tensor_tensor(zval, s_nat[:, :, 0:H], topb, ALU.add))
            step(nc.vector.tensor_scalar(zneg, zval, -(1 - ALPHA), 0.0, ALU.mult, ALU.min))
            step(nc.vector.tensor_scalar(zval, zval, 1 - ALPHA, 0.0, ALU.mult, ALU.min))
            nc.vector.tensor_tensor(nval, s_nat[:, :, H:], topb, ALU.subtract).then_inc(expin_ready, 1)
            cast_adjacency(6, 7)
            largest_v(0, 1, 2, 3)

            def scale_columns():
                step(largest_v(14, 15))
                nc.vector.reduce_max(tops[:, H:H + 1], vmx, AX.X).then_inc(tops_ready, 1)
                dve.wait_ge(topr_ready, 2)
                step(nc.vector.tensor_scalar(gfac[:, 0:1], topr[:, H:H + 1], 1.0, None, ALU.max))
                step(nc.vector.reciprocal(gfac[:, 1:2], gfac[:, 0:1]))
                step(nc.vector.tensor_scalar(gfac[:, 2:3], gfac[:, 1:2], VTOP, None, ALU.mult))
                step(nc.vector.tensor_scalar(gfac[:, 3:4], gfac[:, 1:2], -VTOP, None, ALU.mult))
                dve.wait_ge(exp_ready, 1)
                step(nc.vector.tensor_scalar(bval, bval, gfac[:, 2:3], None, ALU.mult))
                nc.vector.tensor_scalar(nval, nval, gfac[:, 3:4], None, ALU.mult).then_inc(bn_ready, 1)

            def apply_empty_rows(chunks):
                for c in chunks:
                    words = slice(c * P, (c + 1) * P)
                    dve.wait_ge(deg_in_psum, c + 1)
                    step(nc.vector.tensor_scalar(flag8[:, c * 512:(c + 1) * 512], DEG_BANK[c][:, :], 0.0, float(NEG8),
                                                 ALU.is_equal, ALU.mult))
                    step(nc.vector.tensor_tensor(adjw[:, :, words], adjw[:, :, words],
                                                 flagw[:, None, words].to_broadcast([P, T, P]), ALU.bitwise_or))

            return cast_adjacency, largest_v, scale_columns, apply_empty_rows

        def setup_pe(pe):
            def transpose(g):
                for t in range(4 * g, 4 * g + 4):
                    pe.wait_ge(xn_ready, t + 1)
                    if t >= 2:
                        pe.wait_ge(xt_copied, t - 1)
                    for k in range(KD):
                        last = nc.tensor.transpose(bank[t % 2][:, k * P:(k + 1) * P], x_sb[:, t, k * P:(k + 1) * P], ident)
                    last.then_inc(xt_in_psum, 1)

            def project(*tiles):
                for t in tiles:
                    pe.wait_ge(xt_copied, t + 1)
                    if t >= 4:
                        pe.wait_ge(v_copied, t - 3)
                    for k in range(KD):
                        last = nc.tensor.matmul(SEQ_BANK[t % 4][:, :], xnT[:, k, t * P:(t + 1) * P], wseq_sb[:, k, :],
                                                start=(k == 0), stop=(k == KD - 1))
                    last.then_inc(seq_in_psum, 1)

            def scores(c):
                pe.wait_ge(xt_copied, 4 * c + 4)
                if c >= 2:
                    pe.wait_ge(st_copied, c - 1)
                for k in range(KD):
                    last = nc.tensor.matmul(bank[4 + 3 * (c % 2)][0:2 * H, :], wa[:, k, :], xnT[:, k, c * 512:(c + 1) * 512],
                                            start=(k == 0), stop=(k == KD - 1))
                last.then_inc(st_in_psum, 1)

            def degrees(*chunks):
                for c in chunks:
                    for j in range(T):
                        last = nc.tensor.matmul(DEG_BANK[c][:, :], ones16, adj8[:, j, c * 512:(c + 1) * 512],
                                                start=(j == 0), stop=(j == T - 1))
                    last.then_inc(deg_in_psum, 1)

            pe.wait_ge(consts_loaded, 48)
            transpose(0)
            pe.wait_ge(wseq_loaded, 16)
            project(0)
            transpose(1)
            project(1)
            transpose(2)
            project(2)
            transpose(3)
            project(3)
            pe.wait_ge(wa_ready, 1)
            for c in range(4):
                scores(c)
            pe.wait_ge(xt_copied, T)
            project(4)
            pe.wait_ge(st_copied, 4)
            for t in range(T):
                last = nc.tensor.transpose(bank[0][:, t * 2 * H:(t + 1) * 2 * H], sT[:, t * P:(t + 1) * P],
                                           ident[0:2 * H, 0:2 * H])
            last.then_inc(s_in_psum, 1)
            project(5, 6, 7, 8, 9, 10, 11, 12, 13)
            pe.wait_ge(s_copied, 1)
            pe.wait_ge(ones_ready, 1)
            pe.wait_ge(adj_cast, T)
            degrees(0, 1)
            project(14, 15)
            degrees(2)
            pe.wait_ge(v_copied, T)
            degrees(3)

        x1 = hid_t.rearrange("p (t c) -> p t c", t=T)[:, :, 0:D]
        up_sb = place("up_sb", 8448, [KD, SH])
        down_sb = place("down_sb", 16640, [FS, D])
        xhl = [place("xt_high", 41216, [KD, N], f32r), place("xt_low", 33024, [KD, N], f32r)]
        wo_sb = place("wo_sb", 24832, [KD, D])
        xr = place("xr", 26880, [2, D])
        ident2 = place("ident2", 27904, [P])
        bout_sb = place("bout_sb", 28032, [D])
        corr_sb = place("corr_sb", 28544, [E])
        gate_sb = place("gate_sb", 28552, [KD, E])
        lower_sb = place("lower_sb", 28584, [E, E])
        hn = place("hn", 28928, [2, D])
        hT = place("hT", 24832, [2, 2, KD, P], f32r)
        wo_parts = place("wo_parts", 20736, [2, KD, D], f32r)
        bout_parts = place("bout_parts", 29952, [2, D], f32r)
        ones_r = place("ones_r", 28656, [P], f32r)
        pos = place("pos", 30976, [2, D])
        neg = place("neg", 32000, [2, D])
        top[0] = 49408

        def small_at(name, shape, dt=f32):
            words = 1
            for s in shape:
                words *= s
            top[0] += -(-words // 8) * 8
            assert top[0] <= WORDS
            return place(name, top[0] - -(-words // 8) * 8, shape, dt)

        xn2 = small_at("xn2", [2, D])
        gate_hl = small_at("gate_hl", [2, KD, E], f32r)
        rden = small_at("rden", [T, H])
        stat62 = small_at("stat62", [2, 6])
        mv2 = small_at("mv2", [T, 2])
        std2, rstd2 = small_at("std2", [T]), small_at("rstd2", [T])
        minus_half = small_at("minus_half", [1])
        enx = small_at("enx", [T, E])
        RT = 8
        score, sfc, chosen = (small_at(n, [RT, E]) for n in ("score", "sfc", "chosen"))
        gtop, gkeep = (small_at(n, [RT, 2]) for n in ("gtop", "gkeep"))
        gmax, gmin = (small_at(n, [RT, 2, 2]) for n in ("gmax", "gmin"))
        pairs, larger = small_at("pairs", [RT, E, E]), small_at("larger", [RT, E, E])
        wsum = small_at("wsum", [2, RT])
        w_all = small_at("w_all", [T, E])
        wT = place("wT", 26880, [2, 512])[0:E, :, :]
        GT = 4
        WT_BANK = [bank[6], bank[6], bank[7], bank[6]]
        EARLY = 12
        LAGX, LAGG = 3, 5

        c2_loaded, wo_loaded, up_loaded, down_loaded = (sem(n) for n in ("c2_loaded", "wo_loaded", "up_loaded", "down_loaded"))
        xr_loaded = [sem("xr_loaded0"), sem("xr_loaded1")]
        half_ready = sem("half_ready")
        wo_high, wo_low, ht_low, x1_stored_late = sem("wo_high"), sem("wo_low"), sem("ht_low"), sem("x1_stored_late")
        rden_ready, hn_ready, ht_in_psum, ht_copied, y_in_psum, pos_ready, neg_step, e_ready = (sem(n) for n in (
            "rden_ready", "hn_ready", "ht_in_psum", "ht_copied", "y_in_psum", "pos_ready", "neg_step", "e_ready"))
        x1_ready, var2_ready, std2_ready, xn2_ready, xt2_in_psum, xth_copied, xtl_ready, gate_ready = (sem(n) for n in (
            "x1_ready", "var2_ready", "std2_ready", "xn2_ready", "xt2_in_psum", "xth_copied", "xtl_ready", "gate_ready"))
        gate_in_psum, enx_ready, w_ready, wt_in_psum, wt_copied, w_stored, d2, x1_stored = (sem(n) for n in (
            "gate_in_psum", "enx_ready", "w_ready", "wt_in_psum", "wt_copied", "w_stored", "dve_step2",
            "x1_stored"))

        PAIRS = H // 2
        prod_ready, hi_copied, lo_ready, vtmp_free = sem("prod_ready"), sem("hi_copied"), sem("lo_ready"), sem("vtmp_free")
        dve_compared, act_compared, own_masked = sem("dve_compared"), sem("act_compared"), sem("own_masked")
        m_ready, unit_in_psum, sums_ready, sums_free = sem("m_ready"), sem("unit_in_psum"), sem("sums_ready"), sem("sums_free")
        act_passed, pe_passed = sem("act_passed"), sem("pe_passed")
        bias_copied, scaled_step = sem("bias_copied"), sem("scaled_step")
        GROUPS = [(0, 3), (3, 3), (6, 2)]
        GROUP_OF = [(g, i - GROUPS[g][0]) for i in range(IT) for g in [min(i // 3, 2)]]

        with nc.Block() as block:
            @block.sync
            def _(sp):
                setup_loads(sp)
                def stage_s1(p, k):
                    sp.dma_start(s1b[:, k % 2, :],
                                 s1_dram[bass.ds(2 * p + k // 2, 1), (k % 2) * IC:(k % 2 + 1) * IC].to_broadcast([P, IC])
                                 ).then_inc(s1_staged[k % 2], 16)

                def body(p, last):
                    for k in range(4):
                        if not (last and k >= 2):
                            sp.wait_ge(dve_compared, 4 * p + k + 1)
                            sp.wait_ge(act_compared, 4 * p + k + 1)
                            stage_s1(p + (k + 2) // 4, (k + 2) % 4)

                with sp.Fori(0, PAIRS - 1) as p:
                    body(p, False)
                body(PAIRS - 1, True)
                sp.wait_ge(unit_in_psum, UNITS - 3)
                sp.dma_start(wo_sb, w_out.rearrange("(k p) n -> p k n", p=P)).then_inc(wo_loaded, 16)
                sp.dma_start(ident2, ident_in[:, :]).then_inc(c2_loaded, 16)
                sp.dma_start(bout_sb[0:1, :], b_out[None, :]).then_inc(c2_loaded, 16)
                sp.dma_start(corr_sb, corr[None, :].to_broadcast([P, E])).then_inc(c2_loaded, 16)
                sp.dma_start(lower_sb.rearrange("p e f -> p (e f)"), lower_in[None, :].to_broadcast([P, E * E])).then_inc(c2_loaded, 16)
                sp.dma_start(gate_sb, gateT.rearrange("(k p) e -> p k e", p=P)).then_inc(c2_loaded, 16)
                for t in range(2):
                    sp.dma_start(xr[:, t, :], x[t * P:(t + 1) * P, :]).then_inc(xr_loaded[t], 16)

            @block.scalar
            def _(act):
                copy_v = setup_act(act)

                def compare(p, k):
                    b = k // 2
                    if k % 2 == 0:
                        nc.scalar.copy(bias_now[:, b, :], step_bias[:, 2 * p + b, :]).then_inc(bias_copied, 1)
                        act.wait_ge(bias_copied, 2 * p + b + 1)
                    act.wait_ge(s1_staged[k % 2], 32 * p + 16 * (k // 2 + 1))
                    act.sem_inc(act_passed, 1)
                    for j in range(DVE_J, T):
                        last = nc.scalar.activation(m8[:, k, j, :], s1b[:, k % 2, :], ACT.Sigmoid,
                                                    bias=bias_now[:, b, j:j + 1], scale=STEEP, saturate=False)
                    last.then_inc(act_compared, 1)

                def split_high(p, b):
                    act.wait_ge(prod_ready, 2 * p + b + 1)
                    nc.scalar.copy(vs[:, b, :, 0:WD], vtmp).then_inc(hi_copied, 1)

                def body(p, last):
                    for k in range(4):
                        act.wait_ge(unit_in_psum, 4 * p + k + 1)
                        if not last:
                            if k % 2:
                                split_high(p + 1, k // 2)
                            compare(p + 1, k)

                copy_v(4, 5)
                compare(0, 0)
                copy_v(6, 7, 8, 9)
                compare(0, 1)
                copy_v(10, 11, 12, 13)
                copy_v(14, 15)
                split_high(0, 0)
                compare(0, 2)
                split_high(0, 1)
                compare(0, 3)
                with act.Fori(0, PAIRS - 1) as p:
                    body(p, False)
                act.wait_ge(wo_loaded, 16)
                act.wait_ge(c2_loaded, 80)
                act.wait_ge(lo_ready, H)
                act.wait_ge(unit_in_psum, UNITS - 2)
                nc.scalar.copy(wo_parts[:, 0, :, :], wo_sb)
                nc.scalar.copy(bout_parts[0:1, 0, :], bout_sb[0:1, :]).then_inc(wo_high, 1)

            @block.vector
            def _(dve):
                cast_adjacency, largest_v, scale_columns, apply_empty_rows = setup_dve(dve)

                def compare(p, k):
                    dve.wait_ge(s1_staged[k % 2], 32 * p + 16 * (k // 2 + 1))
                    for j in range(DVE_J):
                        last = nc.vector.tensor_scalar(mu8[:, k, j, :], s1b[:, k % 2, :],
                                                       neg_s2[:, 2 * p + k // 2, j:j + 1], float(ONE8), ALU.is_gt, ALU.mult)
                    last.then_inc(dve_compared, 1)

                def mask_own(p, k):
                    cols = slice((k % 2) * IC // 4, (k % 2 + 1) * IC // 4)
                    dve.wait_ge(dve_compared, 4 * p + k + 1)
                    nc.vector.tensor_tensor(mw[:, k, 0:DVE_J, :], mw[:, k, 0:DVE_J, :], adjw[:, 0:DVE_J, cols],
                                            ALU.bitwise_and).then_inc(own_masked, 1)

                def mask_acts(p, k):
                    cols = slice((k % 2) * IC // 4, (k % 2 + 1) * IC // 4)
                    dve.wait_ge(act_compared, 4 * p + k + 1)
                    dve.wait_ge(own_masked, 4 * p + k + 1)
                    nc.vector.tensor_tensor(mw[:, k, DVE_J:, :], mw[:, k, DVE_J:, :], adjw[:, DVE_J:, cols],
                                            ALU.bitwise_and).then_inc(m_ready, 1)

                def collect(p, k):
                    dve.wait_ge(sums_free, 4 * p + k + 1)
                    for g, (t0, n) in enumerate(GROUPS):
                        last = nc.vector.reduce_sum(
                            sums[:, k % 2, t0:t0 + n, :],
                            bank[3 * (k % 2) + g][:, 0:n * WV].rearrange("p (t s c) -> p t c s", t=n, s=2), AX.X)
                    last.then_inc(sums_ready, 1)

                def split_low():
                    dve.wait_ge(wo_high, 1)
                    nc.vector.tensor_tensor(wo_parts[:, 1, :, :], wo_sb, wo_parts[:, 0, :, :].bitcast(f32), ALU.subtract)
                    nc.vector.tensor_tensor(bout_parts[0:1, 1, :], bout_sb[0:1, :], bout_parts[0:1, 0, :].bitcast(f32),
                                            ALU.subtract)
                    nc.vector.tensor_scalar(ones_r[0:1, :], ident2[0:1, :], 0.0, 1.0, ALU.mult, ALU.add).then_inc(wo_low, 1)

                def body(p, last):
                    for k in range(4):
                        if last and k == 3:
                            split_low()
                        dve.wait_ge(unit_in_psum, 4 * p + k + 1)
                        collect(p, k)
                        if not last:
                            compare(p + 1, k)
                            mask_own(p + 1, k)
                        if k == 0:
                            mask_acts(p, 3)
                        elif not last:
                            mask_acts(p + 1, k - 1)

                dve.sem_inc(sums_ready, 2)
                dve.wait_ge(xt_in_psum, T)
                cast_adjacency(8)
                compare(0, 0)
                cast_adjacency(9, 10)
                largest_v(4, 5)
                cast_adjacency(11)
                largest_v(6, 7)
                cast_adjacency(12)
                compare(0, 1)
                cast_adjacency(13)
                largest_v(8, 9)
                cast_adjacency(14)
                largest_v(10, 11)
                cast_adjacency(15)
                largest_v(12, 13)
                apply_empty_rows((0, 1))
                mask_own(0, 0)
                mask_acts(0, 0)
                scale_columns()
                apply_empty_rows((2, 3))
                mask_own(0, 1)
                mask_acts(0, 1)
                compare(0, 2)
                mask_own(0, 2)
                compare(0, 3)
                mask_own(0, 3)
                mask_acts(0, 2)
                with dve.Fori(0, PAIRS - 1) as p:
                    body(p, False)
                body(PAIRS - 1, True)

            @block.gpsimd
            def _(pool):
                setup_pool(pool)
                def build(p, b):
                    h = 2 * p + b
                    pool.wait_ge(vtmp_free, 2 * p + b + 1)
                    vh = v_sb.rearrange("p t (h d) -> p t h d", h=H)[:, :, h, :]
                    for c, val in enumerate((bval, nval)):
                        nc.gpsimd.tensor_tensor(vtmp[:, :, c * W1:c * W1 + DH], vh,
                                                val[:, :, bass.ds(h, 1)].to_broadcast([P, T, DH]), ALU.mult)
                        last = nc.gpsimd.tensor_copy(vtmp[:, :, c * W1 + DH:(c + 1) * W1], val[:, :, bass.ds(h, 1)])
                    last.then_inc(prod_ready, 1)
                    pool.wait_ge(prod_ready, 2 * p + b + 1)
                    pool.wait_ge(hi_copied, 2 * p + b + 1)
                    nc.gpsimd.tensor_tensor(vs[:, b, :, WD:], vtmp, vs[:, b, :, 0:WD], ALU.subtract).then_inc(lo_ready, 1)
                    pool.wait_ge(lo_ready, 2 * p + b + 1)
                    pool.sem_inc(vtmp_free, 1)

                def combine(p, k):
                    h = 2 * p + k // 2
                    tiles = slice((k % 2) * IT, (k % 2 + 1) * IT)
                    pool.wait_ge(sums_ready, 4 * p + k + 3)
                    for c in range(2):
                        last = nc.gpsimd.tensor_tensor(
                            scaled[:, k % 2, :, c * W1:(c + 1) * W1], sums[:, k % 2, :, c * W1:(c + 1) * W1],
                            coef[:, h, tiles, c:c + 1].to_broadcast([P, IT, W1]), ALU.mult)
                    last.then_inc(scaled_step, 1)
                    pool.wait_ge(scaled_step, 4 * p + k + 1)
                    nc.gpsimd.tensor_tensor(hid[:, tiles, h, :], scaled[:, k % 2, :, 0:W1],
                                            scaled[:, k % 2, :, W1:], ALU.add).then_inc(sums_free, 1)

                def body(p, last):
                    for k in range(4):
                        if k % 2 and not last:
                            pool.wait_ge(unit_in_psum, 4 * p + k + 1)
                            build(p + 1, k // 2)
                        combine(p, k)

                pool.sem_inc(sums_free, 2)
                pool.sem_inc(vtmp_free, 1)
                pool.wait_ge(bn_ready, 1)
                build(0, 0)
                build(0, 1)
                with pool.Fori(0, PAIRS - 1) as p:
                    body(p, False)
                body(PAIRS - 1, True)

            @block.tensor
            def _(pe):
                setup_pe(pe)
                with pe.Fori(0, PAIRS) as p:
                    for k in range(4):
                        b = k // 2
                        if k % 2 == 0:
                            pe.wait_ge(lo_ready, 2 * p + b + 1)
                        pe.wait_ge(sums_ready, 4 * p + k + 1)
                        pe.wait_ge(m_ready, 4 * p + k + 1)
                        pe.sem_inc(pe_passed, 1)
                        for i in range(IT):
                            g, slot = GROUP_OF[i]
                            o = bank[3 * (k % 2) + g][:, slot * WV:(slot + 1) * WV]
                            od = o.rearrange("p (s c) -> p s c", s=2)[:, :, W1:WD]
                            for j in range(T):
                                last = nc.tensor.matmul(o, m8[:, k, j, i * P:(i + 1) * P], vs[:, b, j, :],
                                                        start=(j == 0), stop=(j == T - 1))
                                for ja in range(T if j == 0 else 0):
                                    nc.tensor.matmul(
                                        od, adj8[:, ja, (k % 2) * IC + i * P:(k % 2) * IC + (i + 1) * P],
                                        vs[:, b, ja, :].rearrange("p (s c) -> p s c", s=2)[:, :, W1:WD],
                                        start=False, stop=False, skip_group_check=True)
                        last.then_inc(unit_in_psum, 1)

        def project_sync(sp):
            def store(t):
                sp.wait_ge(x1_ready, t + 1)
                sp.dma_start(x1_dram[t * P:(t + 1) * P, :], x1[:, t, :]).then_inc(
                    x1_stored if t < EARLY else x1_stored_late, 16)

            for t in range(2, T):
                store(t - 2)
                sp.dma_start(xr[:, t % 2, :], x[t * P:(t + 1) * P, :]).then_inc(xr_loaded[t % 2], 16)
            sp.wait_ge(x1_stored, 16 * EARLY)
            sp.wait_ge(xn2_ready, EARLY)
            sp.dma_start(fc1_sb, fc1T.rearrange("(k p) l -> p k l", p=P)).then_inc(fc1_loaded, 16)
            for t in range(T - 2, T):
                store(t)
            for g in range(4):
                sp.wait_ge(wt_copied, g + 1)
                sp.dma_start(w_dram[:, g * 512:(g + 1) * 512], wT[:, g % 2, :]).then_inc(w_stored, 16)
                sp.wait_ge(w_stored, 16 * (g + 1))
            sp.wait_ge(x1_stored_late, 16 * (T - EARLY))

        def project_act(act, prepare, unit):
            act.dma_start(up_sb, upT.rearrange("(k p) f -> p k f", p=P)).then_inc(up_loaded, 16)
            half = FS // 2
            act.dma_start(down_sb[:, 0:half, :], downT[0:half * P, :].rearrange("(f p) n -> p f n", p=P)).then_inc(down_loaded, 16)

            def copy_h(t):
                act.wait_ge(ht_in_psum, t + 1)
                if t >= 2:
                    act.wait_ge(y_in_psum, t - 1)
                nc.scalar.copy(hT[:, t % 2, 0, :, :],
                               bank[t % 2][:, :].rearrange("p (k n) -> p k n", k=KD)).then_inc(ht_copied, 1)

            def elu_parts(t):
                act.wait_ge(y_in_psum, t + 1)
                if t >= 2:
                    act.wait_ge(x1_ready, t - 1)
                nc.scalar.activation(neg[:, t % 2, :], bank[2 + t % 2][:, :], ACT.Relu, scale=-1.0).then_inc(neg_step, 1)
                nc.scalar.activation(pos[:, t % 2, :], bank[2 + t % 2][:, :], ACT.Relu).then_inc(pos_ready, 1)
                act.wait_ge(neg_step, t + 1)
                nc.scalar.activation(neg[:, t % 2, :], neg[:, t % 2, :], ACT.Exp, scale=-1.0).then_inc(e_ready, 1)

            def high_of_xt(t):
                act.wait_ge(xt2_in_psum, t + 1)
                nc.scalar.copy(xhl[0][:, :, t * P:(t + 1) * P],
                               bank[4 + t % 2][:, :].rearrange("p (k n) -> p k n", k=KD)).then_inc(xth_copied, 1)

            def exp_gate(g):
                act.wait_ge(gate_in_psum, RT * (g + 1))
                nc.scalar.activation(enx[:, RT * g:RT * g + RT, :],
                                     bank[6 + g][:, 0:RT * E].rearrange("p (t e) -> p t e", t=RT),
                                     ACT.Exp, scale=-1.0).then_inc(enx_ready, 1)

            def copy_w(g):
                act.wait_ge(wt_in_psum, g + 1)
                if g >= 2:
                    act.wait_ge(w_stored, 16 * (g - 1))
                nc.scalar.copy(wT[:, g % 2, :], WT_BANK[g][0:E, :]).then_inc(wt_copied, 1)

            copy_h(0)
            for t in range(T):
                if t + 1 < T:
                    copy_h(t + 1)
                if t == T - 1:
                    prepare()
                elu_parts(t)
                if t >= LAGX:
                    high_of_xt(t - LAGX)
                if t - LAGG == RT - 1:
                    exp_gate(0)
            act.dma_start(down_sb[:, half:, :], downT[half * P:, :].rearrange("(f p) n -> p f n", p=P)).then_inc(down_loaded, 16)
            high_of_xt(T - 3)
            act.wait_ge(x1_ready, T)
            copy_w(0)
            high_of_xt(T - 2)
            unit(0, 0)
            high_of_xt(T - 1)
            copy_w(1)
            unit(0, 1)
            exp_gate(1)
            return copy_w

        def project_pool(pool):
            nc.gpsimd.memset(minus_half, -0.5).then_inc(half_ready, 1)
            pool.wait_ge(half_ready, 1)
            pool.wait_ge(rden_ready, 1)

            def normalise(t):
                if t >= 2:
                    pool.wait_ge(ht_in_psum, t - 1)
                nc.gpsimd.tensor_tensor(hn[:, t % 2, :].rearrange("p (h d) -> p h d", h=H), hid[:, t, :, 0:DH],
                                        rden[:, t, :].rearrange("p (h o) -> p h o", o=1).to_broadcast([P, H, DH]),
                                        ALU.mult).then_inc(hn_ready, 1)

            def root(t):
                pool.wait_ge(var2_ready, t + 1)
                nc.gpsimd.tensor_tensor(rstd2[:, t:t + 1], std2[:, t:t + 1], minus_half, ALU.pow).then_inc(std2_ready, 1)

            for t in range(T + 3):
                if t < T:
                    normalise(t)
                if t >= 3:
                    root(t - 3)

        def project_dve(dve, prepare, unit):
            steps = [0]

            def step(ins):
                steps[0] += 1
                ins.then_inc(d2, 1)
                dve.wait_ge(d2, steps[0])

            def low_of_h(t):
                dve.wait_ge(ht_copied, t + 1)
                nc.vector.tensor_tensor(hT[:, t % 2, 1, :, :], bank[t % 2][:, :].rearrange("p (k n) -> p k n", k=KD),
                                        hT[:, t % 2, 0, :, :].bitcast(f32), ALU.subtract).then_inc(ht_low, 1)

            nc.vector.reciprocal(rden, hid[:, :, :, DH]).then_inc(rden_ready, 1)
            dve.wait_ge(c2_loaded, 80)
            step(nc.vector.tensor_copy(gate_hl[:, 0, :, :], gate_sb))
            nc.vector.tensor_tensor(gate_hl[:, 1, :, :], gate_sb, gate_hl[:, 0, :, :].bitcast(f32),
                                    ALU.subtract).then_inc(gate_ready, 1)

            def residual(t):
                dve.wait_ge(xr_loaded[t % 2], 16 * (t // 2 + 1))
                dve.wait_ge(pos_ready, t + 1)
                dve.wait_ge(hn_ready, t + 1)
                step(nc.vector.scalar_tensor_tensor(out=x1[:, t, :], in0=xr[:, t % 2, :], scalar=-1.0,
                                                    in1=pos[:, t % 2, :], op0=ALU.add, op1=ALU.add))
                dve.wait_ge(e_ready, t + 1)
                nc.vector.tensor_tensor(x1[:, t, :], x1[:, t, :], neg[:, t % 2, :], ALU.add).then_inc(x1_ready, 1)
                dve.wait_ge(x1_ready, t + 1)
                step(nc.vector.bn_stats(stat62[:, t % 2, :], x1[:, t, :]))
                step(nc.vector.bn_aggr(mv2[:, t, :], stat62[:, t % 2, :]))

            def norm(t):
                dve.wait_ge(std2_ready, t + 1)
                if t >= 2:
                    dve.wait_ge(xt2_in_psum, t - 1)
                nc.vector.tensor_scalar(xn2[:, t % 2, :], x1[:, t, :], mv2[:, t, 0:1], rstd2[:, t:t + 1],
                                        ALU.subtract, ALU.mult).then_inc(xn2_ready, 1)

            def low_of_xt(t):
                dve.wait_ge(xth_copied, t + 1)
                cols = slice(t * P, (t + 1) * P)
                nc.vector.tensor_tensor(xhl[1][:, :, cols], bank[4 + t % 2][:, :].rearrange("p (k n) -> p k n", k=KD),
                                        xhl[0][:, :, cols].bitcast(f32), ALU.subtract).then_inc(xtl_ready, 1)

            def route_scores(g):
                tt = nc.vector.tensor_tensor
                dve.wait_ge(enx_ready, g + 1)
                now = enx[:, RT * g:RT * g + RT, :]
                step(nc.vector.tensor_scalar(now, now, 1.0, None, ALU.add))
                step(nc.vector.reciprocal(score, now))
                step(tt(sfc, score, corr_sb[:, None, :].to_broadcast([P, RT, E]), ALU.add))
                s4 = sfc.rearrange("p t (g c) -> p t g c", g=2)
                tt(gmin, s4[:, :, :, 0:2], s4[:, :, :, 2:4], ALU.min)
                step(tt(gmax, s4[:, :, :, 0:2], s4[:, :, :, 2:4], ALU.max))
                tt(gtop, gmax[:, :, :, 0], gmax[:, :, :, 1], ALU.add)
                step(tt(gmin, gmin, gmax, ALU.add))
                for i in range(2):
                    step(tt(gtop, gtop, gmin[:, :, :, i], ALU.max))
                tt(gkeep[:, :, 0], gtop[:, :, 0], gtop[:, :, 1], ALU.is_ge)
                step(tt(gkeep[:, :, 1], gtop[:, :, 0], gtop[:, :, 1], ALU.is_lt))
                step(tt(s4, s4, gkeep.rearrange("p t (g o) -> p t g o", o=1).to_broadcast([P, RT, 2, 4]), ALU.mult))

            def route_choice(g):
                tt = nc.vector.tensor_tensor
                mine = sfc.rearrange("p t (e o) -> p t e o", o=1).to_broadcast([P, RT, E, E])
                other = sfc.rearrange("p t (o f) -> p t o f", o=1).to_broadcast([P, RT, E, E])
                tt(larger, other, mine, ALU.is_gt)
                step(tt(pairs, other, mine, ALU.is_equal))
                step(tt(pairs, pairs, lower_sb[:, None, :, :].to_broadcast([P, RT, E, E]), ALU.mult))
                step(tt(pairs, pairs, larger, ALU.add))
                step(nc.vector.reduce_sum(chosen, pairs, AX.X))

            def route_weights(g):
                tt = nc.vector.tensor_tensor
                step(nc.vector.tensor_scalar(chosen, chosen, 1.5, None, ALU.is_lt))
                step(tt(chosen, chosen, score, ALU.mult))
                step(nc.vector.reduce_sum(wsum[:, 0, :], chosen, AX.X))
                step(nc.vector.tensor_scalar(wsum[:, 0, :], wsum[:, 0, :], 1e-20, None, ALU.add))
                step(nc.vector.reciprocal(wsum[:, 1, :], wsum[:, 0, :]))
                tt(w_all[:, RT * g:RT * g + RT, :], chosen,
                   wsum[:, 1, :].rearrange("p (t o) -> p t o", o=1).to_broadcast([P, RT, E]), ALU.mult).then_inc(w_ready, 1)
                dve.wait_ge(w_ready, g + 1)

            def spread(t):
                nc.vector.tensor_scalar(std2[:, t:t + 1], mv2[:, t, 1:2], EPS, None, ALU.add).then_inc(var2_ready, 1)

            low_of_h(0)
            for t in range(T):
                if t + 1 < T:
                    low_of_h(t + 1)
                if t == T - 1:
                    prepare()
                if t >= 1:
                    residual(t - 1)
                    spread(t - 1)
                if t >= 2:
                    norm(t - 2)
                if t >= LAGX + 1:
                    low_of_xt(t - LAGX - 1)
                if t == RT + LAGG:
                    route_scores(0)
                elif t == RT + LAGG + 1:
                    route_choice(0)
                elif t == RT + LAGG + 2:
                    route_weights(0)
            residual(T - 1)
            spread(T - 1)
            norm(T - 2)
            low_of_xt(T - 4)
            norm(T - 1)
            low_of_xt(T - 3)
            low_of_xt(T - 2)
            unit(0, 0)
            low_of_xt(T - 1)
            unit(0, 1)
            route_scores(1)
            route_choice(1)
            route_weights(1)

        def project_pe(pe, up):
            def transpose_h(t):
                pe.wait_ge(hn_ready, t + 1)
                if t >= 2:
                    pe.wait_ge(ht_low, t - 1)
                for k in range(KD):
                    last = nc.tensor.transpose(bank[t % 2][:, k * P:(k + 1) * P], hn[:, t % 2, k * P:(k + 1) * P], ident2)
                last.then_inc(ht_in_psum, 1)

            def project(t):
                pe.wait_ge(ht_low, t + 1)
                if t >= 2:
                    pe.wait_ge(pos_ready, t - 1)
                for a in range(2):
                    nc.tensor.matmul(bank[2 + t % 2][:, :], ones_r[0:1, :], bout_parts[0:1, a, :], start=(a == 0), stop=False)
                terms = [(k, a, b) for k in range(KD) for a, b in ((0, 0), (0, 1), (1, 0))]
                for n, (k, a, b) in enumerate(terms):
                    last = nc.tensor.matmul(bank[2 + t % 2][:, :], hT[:, t % 2, a, k, :], wo_parts[:, b, k, :],
                                            start=False, stop=(n == len(terms) - 1))
                last.then_inc(y_in_psum, 1)

            def transpose_x(t):
                pe.wait_ge(xn2_ready, t + 1)
                if t >= 2:
                    pe.wait_ge(xtl_ready, t - 1)
                for k in range(KD):
                    last = nc.tensor.transpose(bank[4 + t % 2][:, k * P:(k + 1) * P], xn2[:, t % 2, k * P:(k + 1) * P], ident2)
                last.then_inc(xt2_in_psum, 1)

            def gate(t):
                pe.wait_ge(xtl_ready, t + 1)
                terms = [(k, a, b) for k in range(KD) for a, b in ((0, 0), (0, 1), (1, 0))]
                for n, (k, a, b) in enumerate(terms):
                    last = nc.tensor.matmul(bank[6 + t // RT][:, t % RT * E:(t % RT + 1) * E], xhl[a][:, k, t * P:(t + 1) * P],
                                            gate_hl[:, b, k, :], start=(n == 0), stop=(n == len(terms) - 1))
                last.then_inc(gate_in_psum, 1)

            def transpose_w(g):
                pe.wait_ge(w_ready, g // 2 + 1)
                for q in range(GT):
                    last = nc.tensor.transpose(WT_BANK[g][0:E, q * P:(q + 1) * P], w_all[:, GT * g + q, :], ident2)
                last.then_inc(wt_in_psum, 1)

            pe.wait_ge(c2_loaded, 80)
            transpose_h(0)
            pe.wait_ge(wo_low, 1)
            pe.wait_ge(gate_ready, 1)
            for t in range(T):
                if t + 1 < T:
                    transpose_h(t + 1)
                project(t)
                if t >= LAGX:
                    transpose_x(t - LAGX)
                if t >= LAGG:
                    gate(t - LAGG)
            transpose_x(T - 3)
            gate(T - 5)
            transpose_w(0)
            transpose_x(T - 2)
            gate(T - 4)
            up(0, 0, first=True)
            transpose_x(T - 1)
            gate(T - 3)
            pe.wait_ge(wt_copied, 1)
            transpose_w(1)
            up(0, 1, first=True)
            gate(T - 2)
            gate(T - 1)
            pe.wait_ge(pos_ready, T)
            up(0, 2)
            up(0, 3)
            transpose_w(2)
            pe.wait_ge(wt_copied, 2)
            transpose_w(3)

        GEN = KL + FS + E * KI
        EXP0 = KL + FS
        NS = GEN - KL
        EB = 4
        ew = place("expert_weights", 28928, [EB, 2, KL * INTER])
        hhl = place("h_parts", 24832, [2, 2, TC], f32r)
        sa = place("up_parts", 1024, [2, 2, KD, P], f32r)
        sb_ = place("down_parts", 6144, [2, 2, D], f32r)
        lhl = place("latent_parts", 3072, [2, KL, TC], f32r)
        comb_sb = place("comb_sb", 26880, [KL, TC])
        relu_sb = place("relu_sb", 5120, [2, TC])
        wrow = place("wrow", 27904, [2, TC])
        fc1_sb = place("fc1_sb", 0, [KD, LAT])
        fc2_sb = place("fc2_sb", 49408, [KL, D])
        acc = place("acc", 50432, [TT, D])
        rw = place("relu_weighted", 52480, [TC])
        assert 52480 + TC <= WORDS

        cb, ob = bank[2:4], bank[4:8]

        def up_bank(n):
            if n < KL:
                return bank[n]
            if n < EXP0:
                return bank[n % 4]
            return (bank[0], bank[1], bank[4], bank[5])[(n - EXP0) % 4]

        fc1_loaded, fc2_loaded, lat_ready, sp_passed = sem("fc1_loaded"), sem("fc2_loaded"), sem("lat_ready"), sem("sp_passed")
        ew_loaded = [sem(f"ew_loaded{i}") for i in range(EB)]
        wrow_loaded = [sem("wrow_loaded0"), sem("wrow_loaded1")]
        ea_ready, eb_ready = sem("expert_a_ready"), sem("expert_b_ready")
        a_high, a_ready, b_high, b_ready, up_in_psum, relu_ready, sq_ready, w_scaled, h_high, h_ready, down_done = (
            sem(n) for n in ("a_high", "a_ready", "b_high", "b_ready", "up_in_psum", "relu_ready", "sq_ready", "w_scaled",
                             "h_high", "h_ready", "down_done"))
        expert_used, comb_ready, y2_in_psum, acc_done = (sem(n) for n in ("expert_used", "comb_ready", "y2_in_psum", "acc_done"))
        x1_loaded = [sem(f"x1_loaded{t}") for t in range(TT)]
        stored = [sem(f"stored{t}") for t in range(TT)]

        def a_source(n):
            if n < KL:
                return fc1_sb[:, :, n * P:(n + 1) * P]
            if n < EXP0:
                return up_sb[:, :, (n - KL) * P:(n - KL + 1) * P]
            e, q = divmod(n - EXP0, KI)
            return ew[:, e % EB, 0, :].rearrange("p (k i) -> p k i", k=KL)[:, :, q * P:(q + 1) * P]

        def b_source(n):
            if n < EXP0:
                return down_sb[:, n - KL, :]
            e, q = divmod(n - EXP0, KI)
            return ew[:, e % EB, 1, q * LAT:(q + 1) * LAT]

        def expert_loaded(eng, c, n):
            if n >= EXP0 and (n - EXP0) % KI == 0:
                e = (n - EXP0) // KI
                eng.wait_ge(ew_loaded[e % EB], 32 * (E // EB) * c + 32 * (e // EB + 1))

        with nc.Block() as block:
            @block.sync
            def _(sp):
                project_sync(sp)
                sp.dma_start(fc2_sb, fc2T.rearrange("(k p) n -> p k n", p=P)).then_inc(fc2_loaded, 16)
                with sp.Fori(0, NC_) as c:
                    for t in range(TT):
                        sp.wait_ge(stored[t], 16 * c + 16)
                        sp.sem_inc(sp_passed, 1)
                        sp.dma_start(acc[:, t, :], x1_dram[bass.ds(c * TC + t * P, P), :]).then_inc(x1_loaded[t], 16)
                    for e in range(E):
                        sp.wait_ge(expert_used, E * c + e + 1)
                        sp.dma_start(ew[:, e % EB, 0, :].rearrange("p (k i) -> p k i", k=KL),
                                     w1T[e].rearrange("(k p) i -> p k i", p=P)).then_inc(ew_loaded[e % EB], 16)
                        sp.dma_start(ew[:, e % EB, 1, :].rearrange("p (k l) -> p k l", k=KI),
                                     w2T[e].rearrange("(k p) l -> p k l", p=P)).then_inc(ew_loaded[e % EB], 16)
                        sp.wait_ge(expert_used, E * c + e + 1 + EB - 2)
                        sp.sem_inc(sp_passed, 1)
                        sp.dma_start(wrow[:, e % 2, :],
                                     w_dram[e:e + 1, bass.ds(c * TC, TC)].to_broadcast([P, TC])
                                     ).then_inc(wrow_loaded[e % 2], 16)
                    for t in range(TT):
                        sp.wait_ge(acc_done, 2 * TT * c + 3 * TT + t + 1)
                        sp.sem_inc(sp_passed, 1)
                        sp.dma_start(out[bass.ds(c * TC + t * P, P), :], acc[:, t, :]).then_inc(stored[t], 16)
                for t in range(TT):
                    sp.wait_ge(stored[t], 16 * (NC_ + 1))

            @block.scalar
            def _(act):
                def high_a(c, n):
                    expert_loaded(act, c, n)
                    src = a_source(n)
                    nc.scalar.copy(sa[:, n % 2, 0, 0:src.shape[1], :], src).then_inc(a_high, 1)

                def prepare():
                    act.wait_ge(up_loaded, 16)
                    act.wait_ge(fc1_loaded, 16)
                    act.wait_ge(x1_stored, 16 * EARLY)
                    act.wait_ge(xn2_ready, EARLY)
                    high_a(0, 0)
                    high_a(0, 1)

                def unit(c, n, last=False):
                    act.wait_ge(up_in_psum, GEN * c + n + 1)
                    if n < KL:
                        nc.scalar.copy(lhl[:, 0, n, :], up_bank(n)[:, :]).then_inc(relu_ready, 1)
                    else:
                        act.wait_ge(h_ready, NS * c + n - KL + 1)
                        nc.scalar.activation(relu_sb[:, n % 2, :], up_bank(n)[:, :], ACT.Relu).then_inc(relu_ready, 1)
                    if n + 2 < GEN:
                        high_a(c, n + 2)
                    elif not last:
                        high_a(c + 1, n + 2 - GEN)
                    if n >= KL:
                        m = n - KL
                        act.wait_ge(down_done, NS * c + m + 1)
                        src = b_source(n)
                        nc.scalar.copy(sb_[:, n % 2, 0, 0:src.shape[1]], src).then_inc(b_high, 1)
                        act.wait_ge(sq_ready, NS * c + m + 1)
                        nc.scalar.copy(hhl[:, n % 2, 0, :], relu_sb[:, n % 2, :]).then_inc(h_high, 1)

                def body(c, last):
                    for n in range(KL, GEN):
                        unit(c, n, last)
                    act.wait_ge(down_done, NS * c + NS + 2)
                    for l in range(KL):
                        nc.scalar.copy(comb_sb[:, l, :], cb[l][:, :]).then_inc(comb_ready, 1)
                    if not last:
                        for n in range(KL):
                            unit(c + 1, n)

                copy_w = project_act(act, prepare, unit)
                act.wait_ge(x1_stored_late, 16 * (T - EARLY))
                act.wait_ge(down_loaded, 32)
                copy_w(2)
                copy_w(3)
                with act.Fori(0, NC_ - 1) as c:
                    body(c, False)
                body(NC_ - 1, True)

            @block.vector
            def _(dve):
                dve.sem_inc(h_ready, 2)
                dve.sem_inc(expert_used, EB)
                dve.sem_inc(acc_done, 2 * TT)

                def low_a(n, count):
                    if n >= EXP0:
                        return
                    dve.wait_ge(a_high, count)
                    src = a_source(n)
                    kk = src.shape[1]
                    nc.vector.tensor_tensor(sa[:, n % 2, 1, 0:kk, :], src, sa[:, n % 2, 0, 0:kk, :].bitcast(f32),
                                            ALU.subtract).then_inc(a_ready, 1)

                def prepare():
                    low_a(0, 1)
                    low_a(1, 2)

                def unit(c, n, last=False):
                    m = n - KL
                    r = relu_sb[:, n % 2, :]
                    dve.wait_ge(relu_ready, GEN * c + n + 1)
                    if n < KL:
                        nc.vector.tensor_tensor(lhl[:, 1, n, :], up_bank(n)[:, :], lhl[:, 0, n, :].bitcast(f32),
                                                ALU.subtract).then_inc(lat_ready, 1)
                    elif n < EXP0:
                        nc.vector.tensor_tensor(r, r, r, ALU.mult).then_inc(sq_ready, 1)
                    else:
                        e, q = divmod(n - EXP0, KI)
                        if q == 0:
                            dve.wait_ge(wrow_loaded[e % 2], 16 * (E // 2) * c + 16 * (e // 2 + 1))
                        nc.vector.tensor_tensor(rw, r, wrow[:, e % 2, :], ALU.mult).then_inc(w_scaled, 1)
                        dve.wait_ge(w_scaled, E * KI * c + n - EXP0 + 1)
                        nc.vector.tensor_tensor(r, r, rw, ALU.mult).then_inc(sq_ready, 1)
                    if n + 2 < GEN:
                        low_a(n + 2, GEN * c + n + 3)
                    elif not last:
                        low_a(n + 2 - GEN, GEN * c + n + 3)
                    if n >= KL:
                        if n < EXP0:
                            dve.wait_ge(b_high, NS * c + m + 1)
                            nc.vector.tensor_tensor(sb_[:, n % 2, 1, :], b_source(n), sb_[:, n % 2, 0, :].bitcast(f32),
                                                    ALU.subtract).then_inc(b_ready, 1)
                        dve.wait_ge(h_high, NS * c + m + 1)
                        nc.vector.tensor_tensor(hhl[:, n % 2, 1, :], r, hhl[:, n % 2, 0, :].bitcast(f32),
                                                ALU.subtract).then_inc(h_ready, 1)
                        if n >= EXP0 and (n - EXP0) % KI == KI - 1:
                            dve.wait_ge(h_ready, NS * c + m + 3)
                            dve.wait_ge(eb_ready, E * KI * c + n - EXP0 + 1)
                            dve.sem_inc(expert_used, 1)
                    if n == EXP0:
                        dve.wait_ge(down_done, NS * c + FS + 2)
                        for t in range(TT):
                            dve.wait_ge(x1_loaded[t], 16 * c + 16)
                            nc.vector.tensor_tensor(acc[:, t, :], ob[t][:, :], acc[:, t, :], ALU.add).then_inc(acc_done, 1)

                def body(c, last):
                    for n in range(KL, GEN):
                        unit(c, n, last)
                    if not last:
                        for n in range(KL):
                            unit(c + 1, n)
                    for t in range(TT):
                        dve.wait_ge(y2_in_psum, TT * c + t + 1)
                        dve.wait_ge(acc_done, 2 * TT * c + 2 * TT + t + 1)
                        nc.vector.tensor_tensor(acc[:, t, :], ob[t][:, :], acc[:, t, :], ALU.add).then_inc(acc_done, 1)

                project_dve(dve, prepare, unit)
                dve.wait_ge(x1_stored_late, 16 * (T - EARLY))
                with dve.Fori(0, NC_ - 1) as c:
                    body(c, False)
                body(NC_ - 1, True)

            @block.gpsimd
            def _(pool):
                project_pool(pool)
                for t in range(TT):
                    pool.sem_inc(stored[t], 16)
                with pool.Fori(0, NC_) as c:
                    for n in range(EXP0 - 2, GEN):
                        if n + 2 < GEN:
                            pool.wait_ge(a_high, GEN * c + n + 3)
                            src = a_source(n + 2)
                            nc.gpsimd.tensor_tensor(sa[:, n % 2, 1, 0:KL, :], src, sa[:, n % 2, 0, 0:KL, :].bitcast(f32),
                                                    ALU.subtract).then_inc(ea_ready, 1)
                        if n >= EXP0:
                            pool.wait_ge(b_high, NS * c + n - KL + 1)
                            nc.gpsimd.tensor_tensor(sb_[:, n % 2, 1, 0:LAT], b_source(n), sb_[:, n % 2, 0, 0:LAT].bitcast(f32),
                                                    ALU.subtract).then_inc(eb_ready, 1)

            @block.tensor
            def _(pe):
                TERMS = ((0, 0), (0, 1), (1, 0))
                pe.sem_inc(down_done, 2)

                def up(c, n, first=False):
                    if n in (EXP0, EXP0 + 1):
                        pe.wait_ge(relu_ready, GEN * c + n - 1)
                    elif n in (EXP0 + 2, EXP0 + 3):
                        pe.wait_ge(acc_done, 2 * TT * c + 2 * TT + n - EXP0 - 1)
                    elif n in (KL + 2, KL + 3):
                        pe.wait_ge(lat_ready, KL * c + n - KL - 1)
                    elif n >= KL + 4 or n < KL and not first:
                        pe.wait_ge(relu_ready, GEN * c + n - 3)
                    if n == EXP0:
                        pe.wait_ge(lat_ready, KL * c + KL)
                    if n < EXP0:
                        pe.wait_ge(a_ready, EXP0 * c + n + 1)
                    else:
                        pe.wait_ge(ea_ready, E * KI * c + n - EXP0 + 1)
                    kk = KD if n < EXP0 else KL
                    mm = [(k, a, b) for k in range(kk) for a, b in TERMS]
                    for i, (k, a, b) in enumerate(mm):
                        if n >= EXP0:
                            rhs = lhl[:, b, k, :]
                        elif isinstance(c, int):
                            rhs = xhl[b][:, k, c * TC:(c + 1) * TC]
                        else:
                            rhs = xhl[b][:, k, bass.ds(c * TC, TC)]
                        last = nc.tensor.matmul(up_bank(n)[:, :], sa[:, n % 2, a, k, :], rhs,
                                                start=(i == 0), stop=(i == len(mm) - 1))
                    last.then_inc(up_in_psum, 1)

                def down(c, n):
                    m = n - KL
                    if m == 0:
                        pe.wait_ge(acc_done, 2 * TT * c + 2 * TT)
                    pe.wait_ge(h_ready, NS * c + m + 3)
                    if n < EXP0:
                        pe.wait_ge(b_ready, FS * c + m + 1)
                    else:
                        pe.wait_ge(eb_ready, E * KI * c + n - EXP0 + 1)
                    if n < EXP0:
                        for t in range(TT):
                            for a, b in TERMS:
                                last = nc.tensor.matmul(ob[t][:, :], hhl[:, n % 2, a, t * P:(t + 1) * P], sb_[:, n % 2, b, :],
                                                        start=(m == 0 and (a, b) == TERMS[0]),
                                                        stop=(n == EXP0 - 1 and (a, b) == TERMS[-1]))
                    else:
                        for l in range(KL):
                            for a, b in TERMS:
                                last = nc.tensor.matmul(cb[l][:, :], sb_[:, n % 2, a, l * P:(l + 1) * P], hhl[:, n % 2, b, :],
                                                        start=(n == EXP0 and (a, b) == TERMS[0]),
                                                        stop=(n == GEN - 1 and (a, b) == TERMS[-1]))
                    last.then_inc(down_done, 1)

                def body(c, last):
                    for n in range(KL, GEN):
                        if n + 2 < GEN:
                            up(c, n + 2)
                        elif not last:
                            up(c + 1, n + 2 - GEN)
                        down(c, n)
                    pe.wait_ge(comb_ready, KL * c + KL)
                    for t in range(TT):
                        for l in range(KL):
                            mm = nc.tensor.matmul(ob[t][:, :], comb_sb[:, l, t * P:(t + 1) * P], fc2_sb[:, l, :],
                                                  start=(l == 0), stop=(l == KL - 1))
                        mm.then_inc(y2_in_psum, 1)
                    if not last:
                        for n in range(KL):
                            up(c + 1, n + 2)

                project_pe(pe, up)
                pe.wait_ge(wt_copied, GT)
                pe.wait_ge(fc2_loaded, 16)
                with pe.Fori(0, NC_ - 1) as c:
                    body(c, False)
                body(NC_ - 1, True)


_INS = ["x", "adjT", "w_seq", "a1", "a2", "w_out", "b_out", "gateT", "corr", "w1T", "w2T", "fc1T", "fc2T", "upT",
        "downT", "ident", "lower"]


def kernel(**inputs):
    import numpy as np
    import concourse.bacc as bacc
    from concourse.bass_utils import run_bass_kernel_spmd

    g = {k: np.asarray(v) for k, v in inputs.items()}
    data = {
        "x": g["x"],
        "adjT": g["adj"].T,
        "w_seq": g["L0_gnn_W_seq"],
        "a1": g["L0_gnn_a1"],
        "a2": g["L0_gnn_a2"],
        "w_out": g["L0_gnn_W_out"],
        "b_out": g["L0_gnn_b_out"],
        "gateT": g["L0_ffn_gate"].T,
        "corr": g["L0_ffn_corr_bias"],
        "w1T": g["L0_ffn_w1"].transpose(0, 2, 1),
        "w2T": g["L0_ffn_w2"].transpose(0, 2, 1),
        "fc1T": g["L0_ffn_fc1_w"].T,
        "fc2T": g["L0_ffn_fc2_w"].T,
        "upT": g["L0_ffn_up_w"].T,
        "downT": g["L0_ffn_down_w"].T,
        "ident": np.eye(P, dtype=np.float32),
        "lower": np.tril(np.ones((E, E), np.float32), -1).reshape(-1),
    }
    nc = bacc.Bacc("TRN2", target_bir_lowering=False, num_devices=1)
    arrays, args = {}, []
    for name in _INS:
        a = np.ascontiguousarray(data[name])
        arrays[f"in_{name}"] = a
        args.append(nc.dram_tensor(f"in_{name}", a.shape, mybir.dt.from_np(a.dtype), kind="ExternalInput").ap())
    args.append(nc.dram_tensor("out_0", (N, D), f32, kind="ExternalOutput").ap())
    build(nc, *args)
    r = run_bass_kernel_spmd(nc, [arrays], core_ids=[0])
    return r.results[0]["out_0"]
```
